# Optimizing a Trainium2 kernel written in Bass

```python
import numpy as np
import jax
import jax.numpy as jnp

def _softmax(x, axis=-1):
    return jax.nn.softmax(x, axis=axis)

def _gelu(x):
    return jax.nn.gelu(x, approximate=True)

def _silu(x):
    return jax.nn.silu(x)

def _sigmoid(x):
    return jax.nn.sigmoid(x)

def _layernorm(x, axis=-1, eps=1e-05):
    m = jnp.mean(x, axis=axis, keepdims=True)
    v = jnp.var(x, axis=axis, keepdims=True)
    return (x - m) / jnp.sqrt(v + eps)

def _scatter_add(tgt, idx, src, axis=0):
    return tgt.at[idx].add(src)

def _segment_sum(src, seg, n):
    return jax.ops.segment_sum(src, seg, n)
kernel_name = 'mk_seq_preln_d1_jaxref_r4_17151c'

def setup_inputs(seed: int=0):
    np.random.seed(seed)
    _w = jnp.asarray

    def _L0_attn_setup():
        import jax, jax.numpy as jnp
        import numpy as np
        DIM_MODEL = 512
        DQK = 64
        DV = 64
        NUM_HEADS = 32
        NUM_GROUPS = 8
        H_PER_G = NUM_HEADS // NUM_GROUPS
        ROPE_THETA = 10000.0
        RMS_EPS = 1e-06

        def _rope(x):
            d = x.shape[-1]
            s = x.shape[-2]
            inv_freq = 1.0 / ROPE_THETA ** (jnp.arange(0, d, 2, dtype=jnp.float32) / d)
            ang = jnp.arange(s, dtype=jnp.float32)[:, None] * inv_freq[None, :]
            cos, sin = (jnp.cos(ang), jnp.sin(ang))
            x1, x2 = (x[..., :d // 2], x[..., d // 2:])
            return jnp.concatenate([x1 * cos - x2 * sin, x2 * cos + x1 * sin], axis=-1)
        key = jax.random.key(seed)
        k1, k2, k3 = jax.random.split(key, 3)
        b, s = (2, 512)
        concat = NUM_HEADS * DQK + NUM_GROUPS * (DQK + DV)
        x = jax.random.normal(k1, (b, s, DIM_MODEL), dtype=jnp.float32)
        w_in = jax.random.normal(k2, (concat, DIM_MODEL), dtype=jnp.float32) * DIM_MODEL ** (-0.5)
        w_out = jax.random.normal(k3, (DIM_MODEL, NUM_HEADS * DV), dtype=jnp.float32) * (NUM_HEADS * DV) ** (-0.5)
        rms_w = jnp.ones((DIM_MODEL,), dtype=jnp.float32)
        return {'x': x, 'w_in': w_in, 'w_out': w_out, 'rms_w': rms_w}
    _L0_attn_in = _L0_attn_setup()

    def _L0_ffn_setup():
        import jax, jax.numpy as jnp
        import numpy as np
        D_MODEL = 512
        D_EXPERT = 2048
        EPS = 1e-08

        def ternary_quant(w):
            scale = jnp.mean(jnp.abs(w)) + EPS
            q = jnp.clip(jnp.round(w / scale), -1.0, 1.0) * scale
            return w + jax.lax.stop_gradient(q - w)
        key = jax.random.key(seed)
        k_x, k_up, k_gate, k_down = jax.random.split(key, 4)
        std_in = 1.0 / np.sqrt(D_MODEL)
        std_exp = 1.0 / np.sqrt(D_EXPERT)
        return {'x': jax.random.normal(k_x, (4, 512, D_MODEL), dtype=jnp.float32), 'W_up': jax.random.normal(k_up, (D_EXPERT, D_MODEL), dtype=jnp.float32) * std_in, 'W_gate': jax.random.normal(k_gate, (D_EXPERT, D_MODEL), dtype=jnp.float32) * std_in, 'W_down': jax.random.normal(k_down, (D_MODEL, D_EXPERT), dtype=jnp.float32) * std_exp}
    _L0_ffn_in = _L0_ffn_setup()
    _d = {'L0_attn_x': _L0_attn_in['x'], 'L0_attn_w_in': _L0_attn_in['w_in'], 'L0_attn_w_out': _L0_attn_in['w_out'], 'L0_attn_rms_w': _L0_attn_in['rms_w'], 'L0_ffn_W_up': _L0_ffn_in['W_up'], 'L0_ffn_W_gate': _L0_ffn_in['W_gate'], 'L0_ffn_W_down': _L0_ffn_in['W_down']}
    _x0 = _d['L0_attn_x']
    _d['L0_attn_x'] = jax.random.normal(jax.random.fold_in(jax.random.key(seed), 1), (1, 2048, 512), dtype=_x0.dtype)
    del _x0
    return _d

def reference(L0_attn_x, L0_attn_w_in, L0_attn_w_out, L0_attn_rms_w, L0_ffn_W_up, L0_ffn_W_gate, L0_ffn_W_down):

    def _L0_attn_ref(x, w_in, w_out, rms_w):
        import jax, jax.numpy as jnp
        import numpy as np
        DIM_MODEL = 512
        DQK = 64
        DV = 64
        NUM_HEADS = 32
        NUM_GROUPS = 8
        H_PER_G = NUM_HEADS // NUM_GROUPS
        ROPE_THETA = 10000.0
        RMS_EPS = 1e-06

        def _rope(x):
            d = x.shape[-1]
            s = x.shape[-2]
            inv_freq = 1.0 / ROPE_THETA ** (jnp.arange(0, d, 2, dtype=jnp.float32) / d)
            ang = jnp.arange(s, dtype=jnp.float32)[:, None] * inv_freq[None, :]
            cos, sin = (jnp.cos(ang), jnp.sin(ang))
            x1, x2 = (x[..., :d // 2], x[..., d // 2:])
            return jnp.concatenate([x1 * cos - x2 * sin, x2 * cos + x1 * sin], axis=-1)
        b, s, _ = x.shape
        y = x * jax.lax.rsqrt(jnp.mean(x * x, axis=-1, keepdims=True) + RMS_EPS) * rms_w
        y = jnp.einsum('bsm,cm->bsc', y, w_in)
        cq = NUM_HEADS * DQK
        ck = NUM_GROUPS * DQK
        q, k, v = (y[..., :cq], y[..., cq:cq + ck], y[..., cq + ck:])
        q = q.reshape(b, s, NUM_GROUPS, H_PER_G, DQK).transpose(0, 2, 3, 1, 4)
        k = k.reshape(b, s, NUM_GROUPS, DQK).transpose(0, 2, 1, 3)[:, :, None]
        v = v.reshape(b, s, NUM_GROUPS, DV).transpose(0, 2, 1, 3)[:, :, None]
        q = _rope(q)
        k = _rope(k)
        qk = jnp.einsum('bghsd,bgxpd->bghsp', q, k) * DQK ** (-0.5)
        causal = jnp.tril(jnp.ones((s, s), dtype=bool))
        qk = jnp.where(causal, qk, -jnp.inf)
        attn = jax.nn.softmax(qk, axis=-1)
        o = jnp.einsum('bghsp,bgxpd->bghsd', attn, v)
        o = o.transpose(0, 3, 1, 2, 4).reshape(b, s, NUM_HEADS * DV)
        y = jnp.einsum('bsc,mc->bsm', o, w_out)
        return x + y

    def _L0_ffn_ref(x, W_up, W_gate, W_down):
        import jax, jax.numpy as jnp
        import numpy as np
        D_MODEL = 512
        D_EXPERT = 2048
        EPS = 1e-08

        def ternary_quant(w):
            scale = jnp.mean(jnp.abs(w)) + EPS
            q = jnp.clip(jnp.round(w / scale), -1.0, 1.0) * scale
            return w + jax.lax.stop_gradient(q - w)
        wu = ternary_quant(W_up)
        wg = ternary_quant(W_gate)
        wd = ternary_quant(W_down)
        up = jnp.einsum('bsd,ed->bse', x, wu)
        gate = jnp.einsum('bsd,ed->bse', x, wg)
        hidden = jax.nn.silu(up) * gate
        return jnp.einsum('bse,de->bsd', hidden, wd)
    x = L0_attn_x
    x = x + _L0_attn_ref(_layernorm(x, axis=-1), L0_attn_w_in, L0_attn_w_out, L0_attn_rms_w)
    x = x + _L0_ffn_ref(_layernorm(x, axis=-1), L0_ffn_W_up, L0_ffn_W_gate, L0_ffn_W_down)
    return x

_drawn_inputs = setup_inputs


def setup_inputs(seed=0):
    import zlib

    import numpy as np

    out = dict(_drawn_inputs(seed))
    spreads = {'L0_attn_rms_w': (1.0, 0.6)}
    factors = {}
    for name, (base, spread) in spreads.items():
        noise = np.random.default_rng([zlib.crc32(name.encode()), seed]).standard_normal(out[name].shape)
        drawn = base * np.exp(spread * noise) if base else spread * noise
        out[name] = jnp.asarray(drawn.astype(out[name].dtype))
    for name, factor in factors.items():
        out[name] = (out[name] * factor).astype(out[name].dtype)
    return out
```

```python
import math
from contextlib import ExitStack

import numpy as np
import concourse.bass as bass
from concourse import mybir

F32 = mybir.dt.float32
F16 = mybir.dt.float16
ALU = mybir.AluOpType
ACT = mybir.ActivationFunctionType
AX = mybir.AxisListType

P = 128
S = 2048
D = 512
KT = D // P
TT = S // P
DH = 64
GROUPS = 8
HG = 4
GC = HG * DH + 2 * DH
C = HG * GROUPS * DH
CT = C // P
CHUNK = 512
TPC = CHUNK // P
NCH = S // CHUNK
E = 2048
ET = E // P
LN_EPS = 1e-5
RMS_EPS = 1e-6
Q_EPS = 1e-8
W_SCALE = 256.0
M_SCALE = 16.0
SCALE = DH ** -0.5
VW = DH + 1 + DH + 1
VU = 2 * DH + 1


def ternary_weights(nc, mats, tern_dram, scales_dram):
    N = D * E // P
    PIECE = 2048
    NP = N // PIECE
    with ExitStack() as ctx:
        sb = lambda name, shape, dt: ctx.enter_context(nc.sbuf_tensor(name, shape, dt))
        sem = lambda name: ctx.enter_context(nc.semaphore(name))
        raw = sb("raw", [P, 2, N], F32)
        neg = sb("neg", [P, 2, PIECE], F16)
        tern = sb("tern", [P, 2, N], F16)
        junk = sb("abs_junk", [P, PIECE], F32)
        sums = sb("abs_sums", [P, 3, NP], F32)
        total = sb("abs_total", [P, 3], F32)
        ones = sb("ones_f32", [P, P], F32)
        scale = sb("tern_scale", [P, 3], F32)
        half = sb("tern_half", [P, 3, 2], F32)
        pt = ctx.enter_context(nc.psum_tensor("abs_psum", [P, 512], F32))
        loaded = [sem(f"raw_loaded{m}") for m in range(3)]
        ones_set = sem("ones_set")
        summed = sem("abs_summed")
        totalled = sem("abs_totalled")
        spread = sem("abs_spread")
        scaled = sem("scale_ready")
        negged = sem("neg_ready")
        ready = sem("tern_ready")
        stored = [sem(f"tern_stored{m}") for m in range(4)]
        block = ctx.enter_context(nc.Block())

        @block.sync
        def _(sp):
            for m in range(3):
                if m == 2:
                    sp.wait_ge(ready, NP)
                for i in range(NP):
                    rows = mats[m].shape[1] // NP
                    sp.dma_start(raw[:, m % 2, i * PIECE:(i + 1) * PIECE].rearrange("p (k n) -> p k n", k=rows),
                                 mats[m][:, i * rows:(i + 1) * rows, :]).then_inc(loaded[m], 16)
            for m in range(3):
                sp.wait_ge(ready, NP * (m + 1))
                sp.dma_start(tern_dram[m], tern[:, m % 2, :]).then_inc(stored[m], 16)
            sp.wait_ge(scaled, 9)
            sp.dma_start(scales_dram, scale[:, :]).then_inc(stored[3], 16)
            for s in stored:
                sp.wait_ge(s, 16)

        @block.scalar
        def _(act):
            for m in range(3):
                act.wait_ge(loaded[m], 16 * NP)
                for i in range(NP):
                    if m or i:
                        act.wait_ge(summed, m * NP + i)
                    nc.scalar.activation(junk[:, :], raw[:, m % 2, i * PIECE:(i + 1) * PIECE], ACT.Abs,
                                         accum_out=sums[:, m, i:i + 1]).then_inc(summed, 1)

        @block.tensor
        def _(pe):
            pe.wait_ge(ones_set, 1)
            for m in range(3):
                pe.wait_ge(totalled, m + 1)
                nc.tensor.matmul(pt[:, m:m + 1], ones[:, :], total[:, m:m + 1], start=True,
                                 stop=True).then_inc(spread, 1)

        @block.vector
        def _(dve):
            nc.vector.memset(ones[:, :], 1.0).then_inc(ones_set, 1)
            for m in range(3):
                dve.wait_ge(summed, NP * (m + 1))
                nc.vector.reduce_sum(total[:, m:m + 1], sums[:, m, :], AX.X).then_inc(totalled, 1)
                dve.wait_ge(spread, m + 1)
                nc.vector.tensor_scalar(scale[:, m:m + 1], pt[:, m:m + 1], 1.0 / (D * E), Q_EPS,
                                        ALU.mult, ALU.add).then_inc(scaled, 1)
                dve.wait_ge(scaled, 3 * m + 1)
                nc.vector.tensor_scalar(half[:, m, 0:1], scale[:, m:m + 1], 0.5, None,
                                        ALU.mult).then_inc(scaled, 1)
                nc.vector.tensor_scalar(half[:, m, 1:2], scale[:, m:m + 1], -0.5, None,
                                        ALU.mult).then_inc(scaled, 1)
                dve.wait_ge(scaled, 3 * m + 3)
                if m == 2:
                    dve.wait_ge(stored[0], 16)
                for i in range(NP):
                    cols = slice(i * PIECE, (i + 1) * PIECE)
                    nc.vector.tensor_scalar(neg[:, i % 2, :], raw[:, m % 2, cols], half[:, m, 1:2], None,
                                            ALU.is_lt).then_inc(negged, 1)
                    dve.wait_ge(negged, m * NP + i + 1)
                    nc.vector.scalar_tensor_tensor(tern[:, m % 2, cols], raw[:, m % 2, cols], half[:, m, 0:1],
                                                   neg[:, i % 2, :], ALU.is_gt,
                                                   ALU.subtract).then_inc(ready, 1)


def normalise(nc, x, rms_w, ident_dram, resid_dram, yh, yl):
    x_v = x[0].rearrange("(n p) d -> p n d", p=P)
    r_v = resid_dram.rearrange("(n p) d -> n p d", p=P)
    with ExitStack() as ctx:
        sb = lambda name, shape, dt: ctx.enter_context(nc.sbuf_tensor(name, shape, dt))
        sem = lambda name: ctx.enter_context(nc.semaphore(name))
        ident = sb("n_ident", [P, P], F32)
        rmsw = sb("rmsw", [P, D], F32)
        xin = sb("xin", [P, TT, D], F32)
        stats = sb("n_stats", [P, 2, 6], F32)
        mv = sb("n_mv", [P, 2, 2], F32)
        veps = sb("n_veps", [P, 2], F32)
        rstd = sb("n_rstd", [P, 2], F32)
        ln = sb("n_ln", [P, 2, D], F32)
        z = sb("n_z", [P, TT, D], F32)
        sq = sb("n_sq", [P, 2, D], F32)
        ssq = sb("n_ssq", [P, 2], F32)
        meps = sb("n_meps", [P, 2], F32)
        rrms = sb("n_rrms", [P, 2], F32)
        mhalf = sb("n_mhalf", [P, 1], F32)
        y = sb("n_y", [P, 2, D], F32)
        pt = ctx.enter_context(nc.psum_tensor("n_pt", [P, 2, KT, P], F32))
        const_in = sem("n_const_in")
        x_in = [sem(f"n_x_in{i}") for i in range(NCH)]
        half_set = sem("n_half_set")
        stat = sem("n_stat")
        aggr = sem("n_aggr")
        var_ready = sem("n_var_ready")
        rstd_ready = sem("n_rstd_ready")
        ln_ready = sem("n_ln_ready")
        z_ready = sem("n_z_ready")
        ssq_ready = sem("n_ssq_ready")
        ms_ready = sem("n_ms_ready")
        rrms_ready = sem("n_rrms_ready")
        y_ready = sem("n_y_ready")
        yt_ready = sem("n_yt_ready")
        hi_ready = sem("n_hi_ready")
        lo_ready = sem("n_lo_ready")
        z_out = sem("n_z_out")
        block = ctx.enter_context(nc.Block())

        @block.sync
        def _(sp):
            sp.dma_start(ident[:, :], ident_dram).then_inc(const_in, 16)
            sp.dma_start(rmsw[:, :], rms_w.rearrange("(a d) -> a d", a=1).to_broadcast([P, D])).then_inc(const_in, 16)
            for c in range(NCH):
                tiles = slice(c * TPC, (c + 1) * TPC)
                sp.dma_start(xin[:, tiles, :], x_v[:, tiles, :]).then_inc(x_in[c], 16)
            for n in range(TT):
                sp.wait_ge(z_ready, n + 1)
                sp.dma_start(r_v[n], z[:, n, :]).then_inc(z_out, 16)
            sp.wait_ge(z_out, 16 * TT)

        @block.vector
        def _(dve):
            nc.vector.memset(mhalf[:, :], -0.5).then_inc(half_set, 1)

            def low_part(n):
                dve.wait_ge(hi_ready, n + 1)
                nc.vector.tensor_tensor(yl[:, :, n * P:(n + 1) * P], pt[:, n % 2], yh[:, :, n * P:(n + 1) * P],
                                        ALU.subtract).then_inc(lo_ready, 1)

            dve.wait_ge(const_in, 32)
            for n in range(TT):
                b = n % 2
                dve.wait_ge(x_in[n // TPC], 16)
                if n >= 2:
                    dve.wait_ge(aggr, n - 1)
                nc.vector.bn_stats(stats[:, b, :], xin[:, n, :]).then_inc(stat, 1)
                dve.wait_ge(stat, n + 1)
                if n >= 2:
                    dve.wait_ge(ln_ready, n - 1)
                nc.vector.bn_aggr(mv[:, b, :], stats[:, b, :]).then_inc(aggr, 1)
                dve.wait_ge(aggr, n + 1)
                nc.vector.tensor_scalar(veps[:, b:b + 1], mv[:, b, 1:2], LN_EPS, None, ALU.add).then_inc(var_ready, 1)
                if n:
                    low_part(n - 1)
                dve.wait_ge(rstd_ready, n + 1)
                nc.vector.tensor_scalar(ln[:, b, :], xin[:, n, :], mv[:, b, 0:1], rstd[:, b:b + 1],
                                        ALU.subtract, ALU.mult).then_inc(ln_ready, 1)
                dve.wait_ge(ln_ready, n + 1)
                nc.vector.tensor_tensor(z[:, n, :], xin[:, n, :], ln[:, b, :], ALU.add).then_inc(z_ready, 1)
                dve.wait_ge(rrms_ready, n + 1)
                if n >= 2:
                    dve.wait_ge(yt_ready, n - 1)
                nc.vector.scalar_tensor_tensor(y[:, b, :], ln[:, b, :], rrms[:, b:b + 1], rmsw[:, :],
                                               ALU.mult, ALU.mult).then_inc(y_ready, 1)
            low_part(TT - 1)

        @block.gpsimd
        def _(pool):
            pool.wait_ge(half_set, 1)
            for n in range(TT):
                b = n % 2
                pool.wait_ge(var_ready, n + 1)
                nc.gpsimd.tensor_tensor(rstd[:, b:b + 1], veps[:, b:b + 1], mhalf[:, :], ALU.pow).then_inc(rstd_ready, 1)
                pool.wait_ge(ssq_ready, n + 1)
                nc.gpsimd.tensor_scalar(meps[:, b:b + 1], ssq[:, b:b + 1], 1.0 / D, RMS_EPS, ALU.mult,
                                        ALU.add).then_inc(ms_ready, 1)
                pool.wait_ge(ms_ready, n + 1)
                nc.gpsimd.tensor_tensor(rrms[:, b:b + 1], meps[:, b:b + 1], mhalf[:, :], ALU.pow).then_inc(rrms_ready, 1)

        @block.scalar
        def _(act):
            def high_part(n):
                act.wait_ge(yt_ready, n + 1)
                nc.scalar.activation(yh[:, :, n * P:(n + 1) * P], pt[:, n % 2], ACT.Copy).then_inc(hi_ready, 1)

            for n in range(TT):
                b = n % 2
                if n:
                    high_part(n - 1)
                act.wait_ge(ln_ready, n + 1)
                if n >= 2:
                    act.wait_ge(ssq_ready, n - 1)
                nc.scalar.activation(sq[:, b, :], ln[:, b, :], ACT.Square,
                                     accum_out=ssq[:, b:b + 1]).then_inc(ssq_ready, 1)
            high_part(TT - 1)

        @block.tensor
        def _(pe):
            pe.wait_ge(const_in, 32)
            for n in range(TT):
                pe.wait_ge(y_ready, n + 1)
                if n >= 2:
                    pe.wait_ge(lo_ready, n - 1)
                for k in range(KT):
                    last = nc.tensor.transpose(pt[:, n % 2, k, :], y[:, n % 2, k * P:(k + 1) * P], ident[:, :])
                last.then_inc(yt_ready, 1)


UNITS = NCH * HG
KEY_TILES = [TPC * (u // HG + 1) for u in range(UNITS)]
FIRST_STEP = [sum(KEY_TILES[:u]) for u in range(UNITS + 1)]
STEPS = FIRST_STEP[UNITS]
PIECES = STEPS
PV_LAG = 5
RING = 8
RING32 = 5
SBANKS = 3
OUT_LAG = PV_LAG - 2
TURN_LAG = 2
V_LAG = 3
ROPE_LAG = 5
TILES_KEPT = 4
MROW_SLOT = 2
TURN_PARTS = (0, 1, 2, HG, 3)
POOL_STEPS = [i for i in range(STEPS) if i % 5 in (1, 3)]
DVE_STEPS = [i for i in range(STEPS) if i not in POOL_STEPS]


def step_of(i):
    u = max(w for w in range(UNITS) if FIRST_STEP[w] <= i)
    return u, i - FIRST_STEP[u]


def first_query_tile(c, j):
    return max(0, j - TPC * c)


def score_bank(i):
    return i % SBANKS if i < STEPS - 1 else 1


def bank_before(i):
    return next(p for p in range(i - 1, i - 1 - 2 * SBANKS, -1) if score_bank(p % STEPS) == score_bank(i))


EXP_AHEAD = -min(bank_before(i) for i in range(SBANKS + 1))


def opening():
    idle = [(None, None, [])] * (ROPE_LAG - TURN_LAG)
    out = [(None, ("proj", 0, t), []) for t in range(TPC)] + idle
    out += [(None, ("turn", 0, 0, part), []) for part in TURN_PARTS]
    out += [(None, None, [])]
    out += [(None, ("proj", 0, TPC + i), [(0, 0, i)]) for i in range(KEY_TILES[0])]
    out += [(None, ("mrow", 0, 0) if i == MROW_SLOT else None, [(0, 1, i)]) for i in range(KEY_TILES[1])]
    out += [(None, ("turn", 0, 1, part), []) for part in TURN_PARTS[:-1]]
    return out


def slots():
    jobs = {}

    def spread(units, items):
        free = [FIRST_STEP[u] + j for u in units for j in range(KEY_TILES[u]) if j != MROW_SLOT]
        jobs.update({free[i * len(free) // len(items)]: item for i, item in enumerate(items)})

    projections = lambda ahead, c: [("proj", ahead, TPC * c + t) for t in range(TPC)]
    turns = lambda ahead, c, parts: [("turn", ahead, c, part) for part in parts]
    spread([0], turns(0, 1, TURN_PARTS[-1:]))
    spread([1, 2, 3], projections(0, 2))
    spread([4, 5], turns(0, 2, TURN_PARTS))
    spread([6, 7], projections(0, 3))
    spread([8, 9], turns(0, 3, TURN_PARTS))
    spread([10, 11], projections(1, 0))
    spread([12, 13], turns(1, 0, TURN_PARTS))
    spread([14], projections(1, 1))
    spread([15], turns(1, 1, TURN_PARTS[:-1]))
    for u in range(UNITS):
        jobs[FIRST_STEP[u] + MROW_SLOT] = ("mrow", *divmod(u + 1, UNITS))
    out = []
    for u in range(UNITS):
        n = KEY_TILES[u]
        ahead, w = divmod(u + 2, UNITS)
        m = KEY_TILES[w]
        for j in range(n):
            pieces = [(ahead, w, i) for i in range(j * m // n, (j + 1) * m // n)]
            out.append((FIRST_STEP[u] + j, jobs.get(FIRST_STEP[u] + j), pieces))
    return out


OPENING = opening()
SLOTS = slots()
JOBS = [job for _, job, _ in SLOTS if job]


def side_work(part):
    return [item for _, job, pieces in part for item in [("piece", *p) for p in pieces] + ([job] if job else [])]


OPENING_SIDE = side_work(OPENING)
SLOTS_SIDE = side_work(SLOTS)


def turn_count(c, part):
    return (HG + 1) * c + TURN_PARTS.index(part) + 1


def side_of(part):
    return OPENING_SIDE if part is OPENING else SLOTS_SIDE
OPENING_JOBS = [job for _, job, _ in OPENING if job]
W_SPLIT = {FIRST_STEP[9] + 3 * kt: kt for kt in range(KT)}
TURNS = NCH * (HG + 1)


def slot(part, n):
    return part[n] if 0 <= n < len(part) else (None, None, [])


def attention(nc, w_in_t, cos_dram, sin_dram, ident_dram, half_consts, attn_dram, yh, yl):
    w_v = w_in_t.rearrange("g (k p) n -> p g k n", p=P)
    cos_v = cos_dram.rearrange("(n p) d -> p n d", p=P)
    sin_v = sin_dram.rearrange("(n p) d -> p n d", p=P)
    out_v = attn_dram.rearrange("(c t p) (g d) -> p c t g d", p=P, c=NCH, g=GROUPS)
    with ExitStack() as ctx:
        sb = lambda name, shape, dt: ctx.enter_context(nc.sbuf_tensor(name, shape, dt))
        sem = lambda name: ctx.enter_context(nc.semaphore(name))
        ident = sb("a_ident", [P, P], F32)
        consts = sb("a_consts", [P, 4, P], F16)
        ident16, big, mask_kq, mask_qk = (consts[:, i, :] for i in range(4))
        cos = sb("a_cos", [P, TT, DH], F32)
        sin = sb("a_sin", [P, TT, DH], F32)
        wraw = sb("wraw", [P, KT, GC], F32)
        wh = sb("wh", [P, KT, GC], F16)
        wl = sb("wl", [P, KT, GC], F16)
        proj = sb("proj", [P, TILES_KEPT, GC], F32)
        rope_a = sb("rope_a", [P, TILES_KEPT, HG + 1, DH], F32)
        rope_b = sb("rope_b", [P, TILES_KEPT, HG + 1, DH], F32)
        roped = sb("roped", [P, TPC, HG + 1, 2, DH], F32)
        k_hl = sb("k_hl", [P, 2, S], F16)
        k_h1 = sb("k_h1", [P, 2, S], F16)
        v = sb("v", [P, 2, TT, VW], F16)
        q_hh = sb("q_hh", [P, 2, HG, CHUNK], F16)
        q_lm = sb("q_lm", [P, 2, HG, CHUNK], F16)
        mpart = sb("mpart", [P, 2, TPC, NCH], F32)
        mrow = sb("mrow", [P, 2, TPC], F32)
        mpre = sb("mpre", [P, 2, TPC, P], F16)
        p32 = sb("p32", [P, RING32, CHUNK], F32)
        ph = sb("ph", [P, RING, CHUNK], F16)
        pl = sb("pl", [P, RING, CHUNK], F16)
        osb = sb("osb", [P, 2, TPC, VU], F32)
        osum = sb("osum", [P, 2, TPC, DH], F32)
        rden = sb("rden", [P, 2, TPC], F32)
        onorm = sb("onorm", [P, 2, TPC, HG, DH], F32)
        credit = sb("credit", [P, 16], F32)
        ps = ctx.enter_context(nc.psum_tensor("a_ps", [P, 8, 512], F32))
        sbank = lambda i: ps[:, score_bank(i), :]
        side_bank = lambda part, item: ps[:, 3 + side_of(part).index(item) % 3, :]
        obank = ps[:, 6:8, :]
        o_read = obank[:, :, 0:2 * VW].rearrange("p a (t w) -> p a t w", w=VW)[:, :, :, 0:VU]

        const_in = sem("a_const_in")
        ones_set = sem("ones_set")
        w_loaded = sem("w_loaded")
        w_high = sem("w_high")
        w_low = sem("w_low")
        misc_ready = sem("misc_ready")
        proj_out = sem("proj_out")
        rope_parts = sem("rope_parts")
        v_high = sem("v_high")
        roped_ready = sem("roped_ready")
        turn_high = sem("turn_high")
        turn_low = sem("turn_low")
        scores_ready = sem("scores_ready")
        maxs_ready = sem("maxs_ready")
        maxs_used = sem("maxs_used")
        m_done = sem("m_done")
        m_high = sem("m_high")
        m_ready = sem("m_ready")
        mrow_ready = sem("mrow_ready")
        exp_done = sem("exp_done")
        low_dve = sem("low_dve")
        low_pool = sem("low_pool")
        pv_done = sem("pv_done")
        o_out = sem("o_out")
        o_sum = sem("o_sum")
        o_rden = sem("o_rden")
        o_norm = sem("o_norm")
        o_stored = [sem(f"o_stored{i}") for i in range(2)]
        block = ctx.enter_context(nc.Block())

        def wait_low(eng, g, i):
            if i in POOL_STEPS:
                eng.wait_ge(low_pool, g * len(POOL_STEPS) + POOL_STEPS.index(i) + 1)
            else:
                eng.wait_ge(low_dve, g * len(DVE_STEPS) + DVE_STEPS.index(i) + 1)

        @block.sync
        def _(sp):
            sp.dma_start(ident[:, :], ident_dram).then_inc(const_in, 16)
            sp.dma_start(consts[:, :, :], half_consts).then_inc(const_in, 16)
            sp.dma_start(cos[:, :, :], cos_v).then_inc(const_in, 16)
            sp.dma_start(sin[:, :, :], sin_v).then_inc(const_in, 16)
            load_w = lambda g: sp.dma_start(wraw[:, :, :], w_v[:, bass.ds(g, 1), :, :].rearrange("p a k n -> p (a k) n"))\
                .then_inc(w_loaded, 16)
            load_w(0)
            with sp.Fori(0, GROUPS) as g:
                sp.wait_ge(w_low, (g + 1) * KT)
                load_w(g + 1)
                for c in range(NCH):
                    sp.wait_ge(o_norm, g * UNITS + HG * (c + 1) + 2)
                    sp.dma_start(out_v[:, c, :, bass.ds(g, 1), :].rearrange("p t a d -> p t (a d)"),
                                 onorm[:, c % 2].rearrange("p t h d -> p t (h d)")).then_inc(o_stored[c % 2], 16)
            sp.wait_ge(w_loaded, 16 * (GROUPS + 1))
            for s in o_stored:
                sp.wait_ge(s, 16 * NCH // 2 * GROUPS + 16)

        @block.tensor
        def _(pe):
            pe.wait_ge(const_in, 64)
            pe.wait_ge(ones_set, 5)
            def group(g, par, part):
                def side_read(kind, ahead, *arg):
                    if kind == "piece":
                        pe.wait_ge(maxs_used, (g + ahead) * PIECES + FIRST_STEP[arg[0]] + arg[1] + 1)
                    elif kind == "proj":
                        pe.wait_ge(proj_out, (g + ahead) * TT + arg[0] + 1)
                    elif kind == "turn":
                        pe.wait_ge(turn_low, (g + ahead) * TURNS + turn_count(*arg))
                    else:
                        pe.wait_ge(mrow_ready, (g + ahead) * UNITS + arg[0] + 1 + 2)

                def take_bank(*item):
                    r = side_of(part).index(item)
                    if r >= 3:
                        side_read(*side_of(part)[r - 3])
                    elif part is SLOTS:
                        side_read("piece", 0, 1, KEY_TILES[1] - 1)
                        side_read("mrow", 0, 0)
                        side_read("turn", 0, 1, TURN_PARTS[-2])
                    return side_bank(part, item)

                def project(ahead, t):
                    if t == 0:
                        pe.wait_ge(w_low, (g + ahead + 1) * KT)
                    bank = take_bank("proj", ahead, t)
                    tok = slice(t * P, (t + 1) * P)
                    passes = [(yh, wh), (yh, wl), (yl, wh)]
                    for kt in range(KT):
                        for n, (a, b) in enumerate(passes):
                            last = nc.tensor.matmul(bank[:, 0:GC], a[:, kt, tok], b[:, kt, :],
                                                    start=(kt == 0 and n == 0), stop=(kt == KT - 1 and n == 2))
                    last.then_inc(misc_ready, 1)

                def turn(ahead, c, e):
                    pe.wait_ge(roped_ready, (g + ahead) * TT + TPC * (c + 1) + TILES_KEPT)
                    bank = take_bank("turn", ahead, c, e)
                    for t in range(TPC):
                        last = nc.tensor.transpose(bank[:, t * P:(t + 1) * P],
                                                   roped[:, t, e].rearrange("p a d -> p (a d)"), ident[:, :])
                    last.then_inc(misc_ready, 1)

                def max_rows(ahead, u):
                    pe.wait_ge(m_ready, (g + ahead) * UNITS + u + 1)
                    bank = take_bank("mrow", ahead, u).bitcast(F16)
                    for t in range(TPC):
                        last = nc.tensor.transpose(bank[:, t * P:(t + 1) * P], mpre[:, u % 2, t, :], ident16)
                    last.then_inc(misc_ready, 1)

                def max_piece(ahead, u, i):
                    c, h = divmod(u, HG)
                    t, kk = divmod(i, c + 1)
                    if h == 0 and i == 0:
                        pe.wait_ge(turn_high, (g + ahead) * TURNS + (HG + 1) * (c + 1))
                        pe.wait_ge(turn_low, (g + ahead) * TURNS + (HG + 1) * (c + 1))
                    bank = take_bank("piece", ahead, u, i)
                    width = CHUNK if kk < c else (t + 1) * P
                    last = nc.tensor.matmul(bank[:, 0:width], q_hh[:, c % 2, h, t * P:(t + 1) * P],
                                            k_hl[:, par ^ ahead, kk * CHUNK:kk * CHUNK + width], start=True, stop=(kk < c))
                    if kk == c:
                        last = nc.tensor.matmul(bank[:, width - P:width], big, mask_qk, start=False, stop=True)
                    last.then_inc(maxs_ready, 1)

                def scores(i):
                    u, j = step_of(i)
                    c, h = divmod(u, HG)
                    if j == 0:
                        pe.wait_ge(mrow_ready, g * UNITS + u + 1 + 2)
                    pe.wait_ge(exp_done, g * STEPS + bank_before(i) + 1 + EXP_AHEAD)
                    r = first_query_tile(c, j)
                    diag = j >= TPC * c
                    keys = slice(j * P, (j + 1) * P)
                    out = sbank(i)[:, r * P:CHUNK]
                    nc.tensor.matmul(out, k_hl[:, par, keys], q_hh[:, c % 2, h, r * P:CHUNK], start=True, stop=False)
                    last = nc.tensor.matmul(out, k_h1[:, par, keys], q_lm[:, c % 2, h, r * P:CHUNK],
                                            start=False, stop=not diag)
                    if diag:
                        last = nc.tensor.matmul(sbank(i)[:, r * P:(r + 1) * P], big, mask_kq, start=False, stop=True)
                    last.then_inc(scores_ready, 1)

                def values(i):
                    u, j = step_of(i)
                    c = u // HG
                    if j == 0:
                        pe.wait_ge(o_out, g * UNITS + u + 1)
                    pe.wait_ge(exp_done, g * STEPS + i + 1 + EXP_AHEAD)
                    wait_low(pe, g, i)
                    for t in range(first_query_tile(c, j), TPC):
                        o = obank[:, t // 2, (t % 2) * VW:(t % 2) * VW + VU]
                        nc.tensor.matmul(o, ph[:, i % RING, t * P:(t + 1) * P], v[:, par, j, 0:VU],
                                         start=(j == 0 and t % 2 == 0), stop=False, skip_group_check=True)
                        last = nc.tensor.matmul(o[:, 0:DH + 1], pl[:, i % RING, t * P:(t + 1) * P], v[:, par, j, 0:DH + 1],
                                                start=False, stop=(j == TPC * c + t), skip_group_check=True)
                    last.then_inc(pv_done, 1)

                for step, job, pieces in part:
                    if step is not None:
                        scores(step)
                    if step is not None and step >= PV_LAG:
                        values(step - PV_LAG)
                    for piece in pieces:
                        max_piece(*piece)
                    if job:
                        {"proj": project, "turn": turn, "mrow": max_rows}[job[0]](*job[1:])
                if part is SLOTS:
                    for i in range(STEPS - PV_LAG, STEPS):
                        values(i)

            group(0, 0, OPENING)
            with pe.Fori(0, GROUPS // 2) as pair:
                for par in range(2):
                    group(pair * 2 + par, par, SLOTS)

        @block.scalar
        def _(act):
            act.wait_ge(const_in, 64)
            act.wait_ge(ones_set, 5)
            def group(g, par, part):
                jobs_before = 0 if part is OPENING else len(OPENING_JOBS) + g * len(JOBS)

                def weights_high(ahead, kt):
                    if kt == 0:
                        act.wait_ge(w_loaded, (g + ahead + 1) * 16)
                    nc.scalar.activation(wh[:, kt, :], wraw[:, kt, :], ACT.Copy, scale=W_SCALE).then_inc(w_high, 1)

                def exps(i):
                    u, j = step_of(i)
                    r = first_query_tile(u // HG, j)
                    act.wait_ge(scores_ready, g * STEPS + i + 1)
                    if i >= RING:
                        act.wait_ge(pv_done, g * STEPS + i - RING + 1)
                    if i >= RING32:
                        wait_low(act, g, i - RING32)
                    s = sbank(i)[:, r * P:CHUNK]
                    nc.scalar.activation(p32[:, i % RING32, r * P:CHUNK], s, ACT.Exp, scale=SCALE)
                    nc.scalar.activation(ph[:, i % RING, r * P:CHUNK], s, ACT.Exp, scale=SCALE).then_inc(exp_done, 1)

                def job_out(k, kind, ahead, *arg):
                    act.wait_ge(misc_ready, jobs_before + k + 1)
                    side = par ^ ahead
                    bank = side_bank(part, (kind, ahead, *arg))
                    if kind == "proj":
                        t, = arg
                        act.wait_ge(roped_ready, (g + ahead) * TT + t + 1)
                        nc.scalar.activation(proj[:, t % TILES_KEPT, :], bank[:, 0:GC], ACT.Copy,
                                             scale=1.0 / W_SCALE).then_inc(proj_out, 1)
                    elif kind == "turn":
                        c, e = arg
                        if e < HG:
                            nc.scalar.activation(q_hh[:, c % 2, e, :], bank, ACT.Copy).then_inc(turn_high, 1)
                        else:
                            cols = slice(c * CHUNK, (c + 1) * CHUNK)
                            nc.scalar.activation(k_h1[0:DH, side, cols], bank[0:DH, :], ACT.Copy)
                            nc.scalar.activation(k_hl[:, side, cols], bank, ACT.Copy).then_inc(turn_high, 1)
                    else:
                        c, h = divmod(arg[0], HG)
                        nc.scalar.activation(q_lm[DH:P, c % 2, h, :], bank.bitcast(F16)[DH:P, 0:CHUNK], ACT.Copy)\
                            .then_inc(mrow_ready, 1)

                def unit_out(u):
                    act.wait_ge(pv_done, g * STEPS + FIRST_STEP[u + 1])
                    act.wait_ge(o_norm, g * UNITS + u + 1)
                    nc.scalar.activation(osb[:, u % 2].rearrange("p (a t) w -> p a t w", a=2), o_read,
                                         ACT.Copy).then_inc(o_out, 1)

                if part is OPENING:
                    for kt in range(KT):
                        weights_high(0, kt)
                k = 0
                for n in range(len(part) + 1):
                    step = slot(part, n)[0]
                    if step is not None:
                        exps(step)
                        if step in W_SPLIT:
                            weights_high(1, W_SPLIT[step])
                    if job := slot(part, n - 1)[1]:
                        job_out(k, *job)
                        k += 1
                    if step is not None and step - OUT_LAG in FIRST_STEP[1:]:
                        unit_out(FIRST_STEP.index(step - OUT_LAG) - 1)
                if part is SLOTS:
                    unit_out(UNITS - 1)

            group(0, 0, OPENING)
            with act.Fori(0, GROUPS // 2) as pair:
                for par in range(2):
                    group(pair * 2 + par, par, SLOTS)

        @block.vector
        def _(dve):
            nc.vector.memset(k_h1[DH:P, :, :], 0.0).then_inc(ones_set, 1)
            dve.wait_ge(ones_set, 1)
            nc.vector.memset(k_h1[DH:DH + 2, :, :], M_SCALE).then_inc(ones_set, 1)
            nc.vector.memset(v[:, :, :, :], 1.0).then_inc(ones_set, 1)
            nc.vector.memset(mpre[:, :, :, :], 0.0).then_inc(ones_set, 1)
            for n, (s, ahead) in enumerate(((roped_ready, TILES_KEPT), (mrow_ready, 2), (exp_done, EXP_AHEAD),
                                             (o_out, 1), (o_norm, 2), (o_stored[0], 16), (o_stored[1], 16))):
                nc.vector.memset(credit[:, n:n + 1], 0.0).then_inc(s, ahead)
            nc.vector.memset(credit[:, 15:16], 0.0).then_inc(ones_set, 1)
            dve.wait_ge(const_in, 64)
            def group(g, par, part):
                def weights_low(ahead, kt):
                    dve.wait_ge(w_high, (g + ahead) * KT + kt + 1)
                    nc.vector.scalar_tensor_tensor(wl[:, kt, :], wraw[:, kt, :], W_SCALE, wh[:, kt, :], ALU.mult,
                                                   ALU.subtract).then_inc(w_low, 1)

                def low_part(i):
                    u, j = step_of(i)
                    r = first_query_tile(u // HG, j)
                    cols = slice(r * P, CHUNK)
                    dve.wait_ge(exp_done, g * STEPS + i + 1 + EXP_AHEAD)
                    nc.vector.tensor_tensor(pl[:, i % RING, cols], p32[:, i % RING32, cols], ph[:, i % RING, cols],
                                            ALU.subtract).then_inc(low_dve, 1)

                def reduce_piece(ahead, u, i):
                    gg, c, n = g + ahead, u // HG, FIRST_STEP[u] + i
                    t, kk = divmod(i, c + 1)
                    width = CHUNK if kk < c else (t + 1) * P
                    dve.wait_ge(maxs_ready, gg * PIECES + n + 1)
                    nc.vector.reduce_max(mpart[:, u % 2, t, kk:kk + 1], side_bank(part, ("piece", ahead, u, i))[:, 0:width], AX.X)\
                        .then_inc(maxs_used, 1)
                    if i < KEY_TILES[u] - 1:
                        return
                    dve.wait_ge(maxs_used, gg * PIECES + n + 1)
                    nc.vector.reduce_max(mrow[:, u % 2, :], mpart[:, u % 2, :, 0:c + 1], AX.X).then_inc(m_done, 1)
                    dve.wait_ge(m_done, gg * UNITS + u + 1)
                    dve.wait_ge(mrow_ready, gg * UNITS + u + 1)
                    high, low = mpre[:, u % 2, :, DH:DH + 1], mpre[:, u % 2, :, DH + 1:DH + 2]
                    m = mrow[:, u % 2, :].unsqueeze(2)
                    nc.vector.tensor_scalar(high, m, -1.0 / M_SCALE, None, ALU.mult).then_inc(m_high, 1)
                    dve.wait_ge(m_high, gg * UNITS + u + 1)
                    nc.vector.scalar_tensor_tensor(low, m, -1.0 / M_SCALE, high, ALU.mult,
                                                   ALU.subtract).then_inc(m_ready, 1)

                def split_v(ahead, t):
                    gg, side = g + ahead, par ^ ahead
                    vp = proj[:, t % TILES_KEPT, (HG + 1) * DH:GC]
                    dve.wait_ge(proj_out, gg * TT + t + 1)
                    nc.vector.tensor_copy(v[:, side, t, 0:DH], vp).then_inc(v_high, 1)
                    dve.wait_ge(v_high, gg * TT + t + 1)
                    nc.vector.tensor_tensor(v[:, side, t, DH + 1:VU], vp, v[:, side, t, 0:DH], ALU.subtract)

                def turn_low_part(ahead, c, e):
                    side, bank = par ^ ahead, side_bank(part, ("turn", ahead, c, e))
                    dve.wait_ge(turn_high, (g + ahead) * TURNS + turn_count(c, e))
                    if e < HG:
                        nc.vector.tensor_tensor(q_lm[0:DH, c % 2, e, :], bank[0:DH, :],
                                                q_hh[0:DH, c % 2, e, :], ALU.subtract).then_inc(turn_low, 1)
                    else:
                        cols = slice(c * CHUNK, (c + 1) * CHUNK)
                        nc.vector.tensor_tensor(k_hl[DH:P, side, cols], bank[DH:P, :], k_hl[DH:P, side, cols],
                                                ALU.subtract).then_inc(turn_low, 1)

                def rope_sum(ahead, t):
                    dve.wait_ge(rope_parts, (g + ahead) * TT + t + 1)
                    twice = lambda a: a[:, t % TILES_KEPT].unsqueeze(2).broadcast_to([P, HG + 1, 2, DH])
                    nc.vector.tensor_tensor(roped[:, t % TPC], twice(rope_a), twice(rope_b), ALU.add)\
                        .then_inc(roped_ready, 1)

                def unit_reciprocal(u):
                    dve.wait_ge(o_out, g * UNITS + u + 1 + 1)
                    nc.vector.reciprocal(rden[:, u % 2, :].unsqueeze(2), osb[:, u % 2, :, DH:DH + 1])\
                        .then_inc(o_rden, 1)

                if part is OPENING:
                    for kt in range(KT):
                        weights_low(0, kt)
                for n in range(len(part) + ROPE_LAG):
                    if (job := slot(part, n - ROPE_LAG)[1]) and job[0] == "proj":
                        rope_sum(*job[1:])
                    for piece in slot(part, n - 1)[2]:
                        reduce_piece(*piece)
                    step = slot(part, n - 1)[0]
                    if step is not None:
                        if step in W_SPLIT:
                            weights_low(1, W_SPLIT[step])
                    if slot(part, n - 2)[0] in DVE_STEPS:
                        low_part(slot(part, n - 2)[0])
                    if (job := slot(part, n - TURN_LAG)[1]) and job[0] == "turn":
                        turn_low_part(*job[1:])
                    if (job := slot(part, n - V_LAG)[1]) and job[0] == "proj":
                        split_v(*job[1:])
                    step = slot(part, n - 2)[0]
                    if step is not None and step - OUT_LAG in FIRST_STEP[1:]:
                        unit_reciprocal(FIRST_STEP.index(step - OUT_LAG) - 1)
                if part is SLOTS:
                    unit_reciprocal(UNITS - 1)

            group(0, 0, OPENING)
            with dve.Fori(0, GROUPS // 2) as pair:
                for par in range(2):
                    group(pair * 2 + par, par, SLOTS)

        @block.gpsimd
        def _(pool):
            pool.wait_ge(const_in, 64)
            pool.wait_ge(ones_set, 5)
            def group(g, par, part):
                def low_part(i):
                    u, j = step_of(i)
                    r = first_query_tile(u // HG, j)
                    cols = slice(r * P, CHUNK)
                    pool.wait_ge(exp_done, g * STEPS + i + 1 + EXP_AHEAD)
                    nc.gpsimd.tensor_tensor(pl[:, i % RING, cols], p32[:, i % RING32, cols], ph[:, i % RING, cols],
                                            ALU.subtract).then_inc(low_pool, 1)

                def rope(ahead, t):
                    b, half = t % TILES_KEPT, DH // 2
                    heads = proj[:, b, 0:(HG + 1) * DH].rearrange("p (h d) -> p h d", d=DH)
                    spread = lambda a, w: a.unsqueeze(1).broadcast_to([P, HG + 1, w])
                    pool.wait_ge(proj_out, (g + ahead) * TT + t + 1)
                    pool.wait_ge(roped_ready, (g + ahead) * TT + t + 1)
                    nc.gpsimd.tensor_tensor(rope_a[:, b], heads, spread(cos[:, t, :], DH), ALU.mult)
                    nc.gpsimd.tensor_tensor(rope_b[:, b, :, 0:half], heads[:, :, half:DH],
                                            spread(sin[:, t, 0:half], half), ALU.mult)
                    nc.gpsimd.tensor_tensor(rope_b[:, b, :, half:DH], heads[:, :, 0:half],
                                            spread(sin[:, t, half:DH], half), ALU.mult).then_inc(rope_parts, 1)

                def unit_normalise(u):
                    c, h = divmod(u, HG)
                    pool.wait_ge(o_out, g * UNITS + u + 1 + 1)
                    nc.gpsimd.tensor_tensor(osum[:, u % 2], osb[:, u % 2, :, 0:DH], osb[:, u % 2, :, DH + 1:VU],
                                            ALU.add).then_inc(o_sum, 1)
                    pool.wait_ge(o_sum, g * UNITS + u + 1)
                    pool.wait_ge(o_rden, g * UNITS + u + 1)
                    if h == 0:
                        pool.wait_ge(o_stored[c % 2], g * (16 * NCH // 2) + 16 * (c // 2 + 1))
                    nc.gpsimd.tensor_tensor(onorm[:, c % 2, :, h, :], osum[:, u % 2],
                                            rden[:, u % 2, :].unsqueeze(2).broadcast_to([P, TPC, DH]),
                                            ALU.mult).then_inc(o_norm, 1)

                for n in range(len(part) + 1):
                    if (job := slot(part, n - 1)[1]) and job[0] == "proj":
                        rope(*job[1:])
                    step = slot(part, n - 1)[0]
                    if step is not None:
                        if step in POOL_STEPS:
                            low_part(step)
                        if step - OUT_LAG in FIRST_STEP[1:]:
                            unit_normalise(FIRST_STEP.index(step - OUT_LAG) - 1)
                if part is SLOTS:
                    unit_normalise(UNITS - 1)

            group(0, 0, OPENING)
            with pool.Fori(0, GROUPS // 2) as pair:
                for par in range(2):
                    group(pair * 2 + par, par, SLOTS)


def feed_forward(nc, w_out_t, ident_dram, attn_dram, resid_dram, tern_dram, scales_dram, out):
    w_v = w_out_t.rearrange("(k p) n -> p k n", p=P)
    a_v = attn_dram.rearrange("(n p) c -> p n c", p=P)
    r_v = resid_dram.rearrange("(n p) d -> p n d", p=P)
    o_v = out[0].rearrange("(n p) d -> p n d", p=P)
    with ExitStack() as ctx:
        sb = lambda name, shape, dt: ctx.enter_context(nc.sbuf_tensor(name, shape, dt))
        sem = lambda name: ctx.enter_context(nc.semaphore(name))
        ident = sb("f_ident", [P, P], F32)
        mhalf = sb("f_mhalf", [P, 1], F32)
        credit = sb("f_credit", [P, 16], F32)
        scale = sb("f_scale", [P, 3], F32)
        sgd = sb("f_sgd", [P, 1], F32)
        wraw = sb("f_wraw", [P, 2, D], F32)
        wh = sb("f_wh", [P, CT, D], F16)
        wl = sb("f_wl", [P, CT, D], F16)
        up = sb("f_up", [P, KT, E], F16)
        gate = sb("f_gate", [P, KT, E], F16)
        down = sb("f_down", [P, ET, D], F16)
        att = sb("f_att", [P, 2, C], F32)
        ath = sb("f_ath", [P, CT, P], F16)
        atl = sb("f_atl", [P, CT, P], F16)
        z = sb("f_z", [P, TPC, D], F32)
        x2 = sb("f_x2", [P, TPC, D], F32)
        stats = sb("f_stats", [P, 6], F32)
        mv = sb("f_mv", [P, 2], F32)
        veps = sb("f_veps", [P, 1], F32)
        rstd = sb("f_rstd", [P, 1], F32)
        ln = sb("f_ln", [P, D], F32)
        xh = sb("f_xh", [P, KT, CHUNK], F16)
        xl = sb("f_xl", [P, KT, CHUNK], F16)
        silu = sb("f_silu", [P, 2, CHUNK], F32)
        hid = sb("f_hid", [P, 2, CHUNK], F32)
        hh = sb("f_hh", [P, ET, CHUNK], F16)
        hl = sb("f_hl", [P, ET, CHUNK], F16)
        res = sb("f_res", [P, 2, D], F32)
        ps = ctx.enter_context(nc.psum_tensor("f_ps", [P, 8, 512], F32))
        tbank = lambda i: ps[:, i % 2, :]
        ybank = ps[:, 2, :]
        ubank = lambda i: ps[:, 3 + i % 2, :]
        gbank = lambda i: ps[:, 5 + i % 2, :]
        dbank = ps[:, 7, :]

        const_in = sem("f_const_in")
        w_in = [sem(f"f_w_in{i}") for i in range(2)]
        w_high = sem("f_w_high")
        w_low = sem("f_w_low")
        half_set = sem("f_half_set")
        sgd_ready = sem("f_sgd_ready")
        att_in = [sem(f"f_att_in{i}") for i in range(2)]
        z_in = sem("f_z_in")
        turned = sem("f_turned")
        t_high = sem("f_t_high")
        t_low = sem("f_t_low")
        y_ready = sem("f_y_ready")
        x2_ready = sem("f_x2_ready")
        stat = sem("f_stat")
        aggr = sem("f_aggr")
        var_ready = sem("f_var_ready")
        rstd_ready = sem("f_rstd_ready")
        ln_ready = sem("f_ln_ready")
        up_ready = sem("f_up_ready")
        gate_ready = sem("f_gate_ready")
        silu_ready = sem("f_silu_ready")
        hid_ready = sem("f_hid_ready")
        h_high = sem("f_h_high")
        h_low = sem("f_h_low")
        down_ready = sem("f_down_ready")
        res_ready = sem("f_res_ready")
        res_out = [sem(f"f_res_out{i}") for i in range(2)]
        credits = sem("f_credits")
        block = ctx.enter_context(nc.Block())
        BANKS = CT // 4 + 1
        T_AHEAD = 2 * BANKS - CT // 4 + 1

        @block.sync
        def _(sp):
            sp.dma_start(ident[:, :], ident_dram).then_inc(const_in, 16)
            sp.dma_start(scale[:, :], scales_dram).then_inc(const_in, 16)
            sp.dma_start(up[:, :, :], tern_dram[0].rearrange("p (k n) -> p k n", k=KT)).then_inc(const_in, 16)
            sp.dma_start(gate[:, :, :], tern_dram[1].rearrange("p (k n) -> p k n", k=KT)).then_inc(const_in, 16)
            sp.dma_start(down[:, :, :], tern_dram[2].rearrange("p (k n) -> p k n", k=ET)).then_inc(const_in, 16)
            for k in range(CT):
                if k >= 2:
                    sp.wait_ge(w_low, k - 1)
                sp.dma_start(wraw[:, k % 2, :], w_v[:, k, :]).then_inc(w_in[k % 2], 16)
            sp.wait_ge(credits, 1)
            with sp.Fori(0, NCH) as c:
                sp.wait_ge(res_ready, c * TPC + 1)
                sp.dma_start(z[:, :, :], r_v[:, bass.ds(c * TPC, TPC), :]).then_inc(z_in, 16)
                for t in range(TPC):
                    sp.wait_ge(t_low, (c * TPC + t - 2) * BANKS + CT // 4 + T_AHEAD)
                    sp.dma_start(att[:, t % 2, :], a_v[:, bass.ds(c * TPC + t, 1), :].rearrange("p a c -> p (a c)"))\
                      .then_inc(att_in[t % 2], 16)
                for t in range(TPC):
                    sp.wait_ge(res_ready, c * TPC + t + 2)
                    sp.dma_start(o_v[:, bass.ds(c * TPC + t, 1), :].rearrange("p a d -> p (a d)"), res[:, t % 2, :])\
                      .then_inc(res_out[t % 2], 16)
            for s in res_out:
                sp.wait_ge(s, 16 * TT // 2 + 16)

        @block.tensor
        def _(pe):
            pe.wait_ge(const_in, 80)
            pe.wait_ge(credits, 1)
            pe.wait_ge(w_low, CT)
            with pe.Fori(0, NCH) as c:
                for t in range(TPC):
                    pe.wait_ge(att_in[t % 2], c * 32 + 16 * (t // 2 + 1))
                    for q in range(CT // 4):
                        n = t * BANKS + q
                        pe.wait_ge(t_low, c * (TPC * BANKS) + n - 1 + T_AHEAD)
                        for k in range(4):
                            last = nc.tensor.transpose(tbank(n)[:, k * P:(k + 1) * P],
                                                       att[:, t % 2, (4 * q + k) * P:(4 * q + k + 1) * P], ident[:, :])
                        last.then_inc(turned, 1)
                    pe.wait_ge(t_low, c * (TPC * BANKS) + t * BANKS + CT // 4 + T_AHEAD)
                    for k in range(CT):
                        for n, (a, b) in enumerate([(ath, wh), (ath, wl), (atl, wh)]):
                            last = nc.tensor.matmul(ybank, a[:, k, :], b[:, k, :], start=(k == 0 and n == 0),
                                                    stop=(k == CT - 1 and n == 2))
                    last.then_inc(y_ready, 1)
                    n = t * BANKS + CT // 4
                    pe.wait_ge(ln_ready, c * TPC + t + 1)
                    for k in range(KT):
                        last = nc.tensor.transpose(tbank(n)[:, k * P:(k + 1) * P], ln[:, k * P:(k + 1) * P], ident[:, :])
                    last.then_inc(turned, 1)
                pe.wait_ge(t_low, (c + 1) * (TPC * BANKS) + T_AHEAD)
                for e in range(ET):
                    cols = slice(e * P, (e + 1) * P)
                    pe.wait_ge(silu_ready, c * ET + e + 1)
                    for k in range(KT):
                        for x in (xh, xl):
                            last = nc.tensor.matmul(ubank(e), up[:, k, cols], x[:, k, :], start=(k == 0 and x is xh),
                                                    stop=(k == KT - 1 and x is xl))
                    last.then_inc(up_ready, 1)
                    pe.wait_ge(hid_ready, c * ET + e + 1)
                    for k in range(KT):
                        for x in (xh, xl):
                            last = nc.tensor.matmul(gbank(e), gate[:, k, cols], x[:, k, :], start=(k == 0 and x is xh),
                                                    stop=(k == KT - 1 and x is xl))
                    last.then_inc(gate_ready, 1)
                pe.wait_ge(h_low, (c + 1) * ET + 2)
                for t in range(TPC):
                    pe.wait_ge(res_ready, c * TPC + t + 1)
                    for e in range(ET):
                        for h in (hh, hl):
                            last = nc.tensor.matmul(dbank, h[:, e, t * P:(t + 1) * P], down[:, e, :],
                                                    start=(e == 0 and h is hh), stop=(e == ET - 1 and h is hl))
                    last.then_inc(down_ready, 1)

        @block.scalar
        def _(act):
            act.wait_ge(const_in, 80)
            for k in range(CT):
                act.wait_ge(w_in[k % 2], 16 * (k // 2 + 1))
                nc.scalar.activation(wh[:, k, :], wraw[:, k % 2, :], ACT.Copy, scale=W_SCALE).then_inc(w_high, 1)
            act.wait_ge(credits, 1)
            with act.Fori(0, NCH) as c:
                for t in range(TPC):
                    for q in range(BANKS):
                        n = t * BANKS + q
                        act.wait_ge(turned, c * (TPC * BANKS) + n + 1)
                        if q < CT // 4:
                            if q == 0:
                                act.wait_ge(y_ready, c * TPC + t + 1)
                            out_h = ath[:, 4 * q:4 * q + 4, :]
                        else:
                            out_h = xh[:, :, t * P:(t + 1) * P]
                        nc.scalar.activation(out_h, tbank(n).rearrange("p (k n) -> p k n", k=4), ACT.Copy)\
                            .then_inc(t_high, 1)
                for e in range(ET):
                    act.wait_ge(up_ready, c * ET + e + 1)
                    act.wait_ge(hid_ready, c * ET + e + 1)
                    nc.scalar.activation(silu[:, e % 2, :], ubank(e), ACT.Silu, scale=scale[:, 0:1])\
                        .then_inc(silu_ready, 1)
                    act.wait_ge(hid_ready, c * ET + e + 1 + 2)
                    nc.scalar.activation(hh[:, e, :], hid[:, e % 2, :], ACT.Copy).then_inc(h_high, 1)

        @block.vector
        def _(dve):
            nc.vector.memset(mhalf[:, :], -0.5).then_inc(half_set, 1)
            for n, (s, ahead) in enumerate(((t_low, T_AHEAD), (y_ready, 1), (silu_ready, 2), (hid_ready, 2), (h_low, 2), (res_ready, 1), (res_out[0], 16), (res_out[1], 16))):
                nc.vector.memset(credit[:, n:n + 1], 0.0).then_inc(s, ahead)
            nc.vector.memset(credit[:, 15:16], 0.0).then_inc(credits, 1)
            dve.wait_ge(const_in, 80)
            nc.vector.tensor_tensor(sgd[:, :], scale[:, 1:2], scale[:, 2:3], ALU.mult).then_inc(sgd_ready, 1)
            for k in range(CT):
                dve.wait_ge(w_high, k + 1)
                nc.vector.scalar_tensor_tensor(wl[:, k, :], wraw[:, k % 2, :], W_SCALE, wh[:, k, :], ALU.mult,
                                               ALU.subtract).then_inc(w_low, 1)
            dve.wait_ge(sgd_ready, 1)
            with dve.Fori(0, NCH) as c:
                def split_low(n, out_l, high):
                    dve.wait_ge(t_high, c * (TPC * BANKS) + n + 1)
                    nc.vector.tensor_tensor(out_l, tbank(n).rearrange("p (k n) -> p k n", k=4), high,
                                            ALU.subtract).then_inc(t_low, 1)

                dve.wait_ge(z_in, c * 16 + 16)
                for t in range(TPC):
                    for q in range(CT // 4):
                        split_low(t * BANKS + q, atl[:, 4 * q:4 * q + 4, :], ath[:, 4 * q:4 * q + 4, :])
                    i = c * TPC + t
                    dve.wait_ge(y_ready, i + 1 + 1)
                    nc.vector.scalar_tensor_tensor(x2[:, t, :], ybank, 1.0 / W_SCALE, z[:, t, :], ALU.mult,
                                                   ALU.add).then_inc(x2_ready, 1)
                    dve.wait_ge(x2_ready, i + 1)
                    nc.vector.bn_stats(stats[:, :], x2[:, t, :]).then_inc(stat, 1)
                    dve.wait_ge(stat, i + 1)
                    nc.vector.memset(credit[:, 14:15], 0.0)
                    nc.vector.bn_aggr(mv[:, :], stats[:, :]).then_inc(aggr, 1)
                    dve.wait_ge(aggr, i + 1)
                    nc.vector.tensor_scalar(veps[:, :], mv[:, 1:2], LN_EPS, None, ALU.add).then_inc(var_ready, 1)
                    dve.wait_ge(rstd_ready, i + 1)
                    nc.vector.tensor_scalar(ln[:, :], x2[:, t, :], mv[:, 0:1], rstd[:, :], ALU.subtract,
                                            ALU.mult).then_inc(ln_ready, 1)
                    split_low(t * BANKS + CT // 4, xl[:, :, t * P:(t + 1) * P], xh[:, :, t * P:(t + 1) * P])
                for e in range(ET):
                    dve.wait_ge(silu_ready, c * ET + e + 1 + 2)
                    dve.wait_ge(gate_ready, c * ET + e + 1)
                    dve.wait_ge(h_low, c * ET + e + 1)
                    nc.vector.tensor_tensor(hid[:, e % 2, :], silu[:, e % 2, :], gbank(e), ALU.mult)\
                        .then_inc(hid_ready, 1)
                for t in range(TPC):
                    i = c * TPC + t
                    dve.wait_ge(down_ready, i + 1)
                    dve.wait_ge(res_out[t % 2], c * (16 * TPC // 2) + 16 * (t // 2 + 1))
                    nc.vector.scalar_tensor_tensor(res[:, t % 2, :], dbank, sgd[:, :], x2[:, t, :], ALU.mult,
                                                   ALU.add).then_inc(res_ready, 1)

        @block.gpsimd
        def _(pool):
            pool.wait_ge(half_set, 1)
            pool.wait_ge(credits, 1)
            with pool.Fori(0, NCH) as c:
                for t in range(TPC):
                    pool.wait_ge(var_ready, c * TPC + t + 1)
                    nc.gpsimd.tensor_tensor(rstd[:, :], veps[:, :], mhalf[:, :], ALU.pow).then_inc(rstd_ready, 1)
                for e in range(ET):
                    pool.wait_ge(h_high, c * ET + e + 1)
                    nc.gpsimd.tensor_tensor(hl[:, e, :], hid[:, e % 2, :], hh[:, e, :], ALU.subtract).then_inc(h_low, 1)


def build(nc, x, w_in_t, w_out_t, rms_w, up_t, gate_t, down_t, cos, sin, ident, half_consts, out):
    resid = nc.dram_tensor("resid_scratch", (S, D), F32, kind="Internal").ap()
    attn = nc.dram_tensor("attn_scratch", (S, C), F32, kind="Internal").ap()
    tern = [nc.dram_tensor(f"tern_scratch{m}", (P, D * E // P), F16, kind="Internal").ap() for m in range(3)]
    scales = nc.dram_tensor("scales_scratch", (P, 3), F32, kind="Internal").ap()
    mats = [w.rearrange("(k p) n -> p k n", p=P) for w in (up_t, gate_t, down_t)]
    ternary_weights(nc, mats, tern, scales)
    with nc.sbuf_tensor("yh", [P, KT, S], F16) as yh, nc.sbuf_tensor("yl", [P, KT, S], F16) as yl:
        normalise(nc, x, rms_w, ident, resid, yh, yl)
        attention(nc, w_in_t, cos, sin, ident, half_consts, attn, yh, yl)
    feed_forward(nc, w_out_t, ident, attn, resid, tern, scales, out)


def shape_constants():
    inv_freq = (np.float32(1.0) / np.float32(10000.0) ** (np.arange(0, DH, 2, dtype=np.float32) / np.float32(DH)))
    ang = np.arange(S, dtype=np.float32)[:, None] * inv_freq.astype(np.float32)[None, :]
    cos, sin = np.cos(ang).astype(np.float32), np.sin(ang).astype(np.float32)
    big = np.float16(30000.0)
    key, query = np.arange(P)[:, None], np.arange(P)[None, :]
    half = np.stack([np.eye(P), np.eye(P) * big, np.where(key > query, -big, 0), np.where(query > key, -big, 0)], axis=1)
    return (np.concatenate([cos, cos], 1), np.concatenate([-sin, sin], 1), np.eye(P, dtype=np.float32),
            half.astype(np.float16))


def kernel(L0_attn_x, L0_attn_w_in, L0_attn_w_out, L0_attn_rms_w, L0_ffn_W_up, L0_ffn_W_gate, L0_ffn_W_down):
    import concourse.bacc as bacc
    from concourse.bass_utils import run_bass_kernel_spmd

    w = np.asarray(L0_attn_w_in)
    nq, nk = C, GROUPS * DH
    by_group = np.concatenate([w[:nq].reshape(GROUPS, HG * DH, D), w[nq:nq + nk].reshape(GROUPS, DH, D),
                               w[nq + nk:].reshape(GROUPS, DH, D)], axis=1)
    by_group = np.concatenate([by_group, by_group[:1]])
    cos, sin, ident, half = shape_constants()
    arrays = {
        "x": np.asarray(L0_attn_x), "w_in_t": by_group.transpose(0, 2, 1), "w_out_t": np.asarray(L0_attn_w_out).T,
        "rms_w": np.asarray(L0_attn_rms_w), "up_t": np.asarray(L0_ffn_W_up).T, "gate_t": np.asarray(L0_ffn_W_gate).T,
        "down_t": np.asarray(L0_ffn_W_down).T, "cos": cos, "sin": sin, "ident": ident, "half_consts": half,
    }
    arrays = {n: np.ascontiguousarray(a) for n, a in arrays.items()}
    nc = bacc.Bacc("TRN2", target_bir_lowering=False, num_devices=1)
    args = [nc.dram_tensor(n, a.shape, mybir.dt.from_np(a.dtype), kind="ExternalInput").ap() for n, a in arrays.items()]
    out = nc.dram_tensor("out", (1, S, D), F32, kind="ExternalOutput").ap()
    build(nc, *args, out)
    return run_bass_kernel_spmd(nc, [arrays], core_ids=[0]).results[0]["out"]
```

```python
import math
from contextlib import ExitStack

import numpy as np
import concourse.bass as bass
from concourse import mybir

F32 = mybir.dt.float32
F16 = mybir.dt.float16
ALU = mybir.AluOpType
ACT = mybir.ActivationFunctionType
AX = mybir.AxisListType

P = 128
S = 2048
D = 512
KT = D // P
TT = S // P
DH = 64
GROUPS = 8
HG = 4
GC = HG * DH + 2 * DH
C = HG * GROUPS * DH
CT = C // P
CHUNK = 512
TPC = CHUNK // P
NCH = S // CHUNK
E = 2048
ET = E // P
NW = D * E // P
NQ = 4
QC = C // NQ
QN = NW // NQ
LN_EPS = 1e-5
RMS_EPS = 1e-6
Q_EPS = 1e-8
W_SCALE = 256.0
M_SCALE = 16.0
SCALE = DH ** -0.5
VW = DH + 1 + DH + 1
VU = 2 * DH + 1


def normalise(nc, x, rms_w, resid_dram, yh, yl, ident, ahead):
    x_v = x[0].rearrange("(n p) d -> p n d", p=P)
    r_v = resid_dram.rearrange("(n p) d -> p n d", p=P)
    with ExitStack() as ctx:
        sb = lambda name, shape, dt: ctx.enter_context(nc.sbuf_tensor(name, shape, dt))
        sem = lambda name: ctx.enter_context(nc.semaphore(name))
        rmsw = sb("rmsw", [P, D], F32)
        xin = sb("xin", [P, TT, D], F32)
        stats = sb("n_stats", [P, 2, TPC, 6], F32)
        mv = sb("n_mv", [P, 2, TPC, 2], F32)
        veps = sb("n_veps", [P, 2, TPC], F32)
        rstd = sb("n_rstd", [P, 2, TPC], F32)
        ln = sb("n_ln", [P, 2, TPC, D], F32)
        sq = sb("n_sq", [P, 2, D], F32)
        ssq = sb("n_ssq", [P, 2, TPC], F32)
        meps = sb("n_meps", [P, 2, TPC], F32)
        rrms = sb("n_rrms", [P, 2, TPC], F32)
        mhalf = sb("n_mhalf", [P, TPC], F32)
        y = sb("n_y", [P, TPC, D], F32)
        pt = ctx.enter_context(nc.psum_tensor("n_pt", [P, TPC, KT, P], F32))
        ident_in = sem("n_ident_in")
        rmsw_in = sem("n_rmsw_in")
        x_in = [sem(f"n_x_in{i}") for i in range(NCH)]
        x_first = [sem(f"n_x_first{t}") for t in range(TPC)]
        ahead_in = sem("n_ahead_in")
        half_set = sem("n_half_set")
        stat = sem("n_stat")
        aggr = sem("n_aggr")
        var_ready = sem("n_var_ready")
        rstd_ready = sem("n_rstd_ready")
        ln_ready = sem("n_ln_ready")
        z_ready = sem("n_z_ready")
        ssq_ready = sem("n_ssq_ready")
        ms_ready = sem("n_ms_ready")
        rrms_ready = sem("n_rrms_ready")
        y_ready = sem("n_y_ready")
        yt_ready = sem("n_yt_ready")
        hi_ready = sem("n_hi_ready")
        lo_ready = sem("n_lo_ready")
        z_out = sem("n_z_out")
        block = ctx.enter_context(nc.Block())
        tiles = lambda b: slice(b * TPC, (b + 1) * TPC)

        @block.sync
        def _(sp):
            for c in range(NCH):
                if c:
                    sp.dma_start(xin[:, tiles(c), :], x_v[:, tiles(c), :]).then_inc(x_in[c], 16)
                else:
                    for t in range(TPC):
                        sp.dma_start(xin[:, t, :], x_v[:, t, :]).then_inc(x_first[t], 16)
                    sp.dma_start(ident[:, :], ahead[0][1]).then_inc(ident_in, 16)
                    sp.dma_start(rmsw[:, :], rms_w.rearrange("(a d) -> a d", a=1).to_broadcast([P, D]))\
                        .then_inc(rmsw_in, 16)
            for to, source in ahead[1:]:
                sp.dma_start(to, source).then_inc(ahead_in, 16)
            for b in range(NCH):
                sp.wait_ge(z_ready, TPC * (b + 1))
                sp.dma_start(r_v[:, tiles(b), :], xin[:, tiles(b), :]).then_inc(z_out, 16)
            sp.wait_ge(z_out, 16 * NCH)
            sp.wait_ge(ahead_in, 16 * (len(ahead) - 1))

        @block.vector
        def _(dve):
            nc.vector.memset(mhalf[:, :], -0.5).then_inc(half_set, 1)

            def statistics(b):
                if b:
                    dve.wait_ge(x_in[b], 16)
                for t in range(TPC):
                    if b == 0:
                        dve.wait_ge(x_first[t], 16)
                    nc.vector.bn_stats(stats[:, b % 2, t, :], xin[:, b * TPC + t, :]).then_inc(stat, 1)
                dve.wait_ge(stat, TPC * (b + 1))
                for t in range(TPC):
                    nc.vector.bn_aggr(mv[:, b % 2, t, :], stats[:, b % 2, t, :]).then_inc(aggr, 1)
                dve.wait_ge(aggr, TPC * (b + 1))
                nc.vector.tensor_scalar(veps[:, b % 2, :].unsqueeze(2), mv[:, b % 2, :, 1:2], LN_EPS, None,
                                        ALU.add).then_inc(var_ready, 1)

            def layer_norm(b):
                dve.wait_ge(rstd_ready, b + 1)
                if b >= 2:
                    dve.wait_ge(z_ready, TPC * (b - 1))
                    dve.wait_ge(ssq_ready, TPC * (b - 1))
                for t in range(TPC):
                    nc.vector.tensor_scalar(ln[:, b % 2, t, :], xin[:, b * TPC + t, :], mv[:, b % 2, t, 0:1],
                                            rstd[:, b % 2, t:t + 1], ALU.subtract, ALU.mult).then_inc(ln_ready, 1)

            statistics(0)
            layer_norm(0)
            dve.wait_ge(rmsw_in, 16)
            for b in range(NCH):
                if b < NCH - 1:
                    statistics(b + 1)
                dve.wait_ge(ln_ready, TPC * (b + 1))
                dve.wait_ge(rrms_ready, b + 1)
                for t in range(TPC):
                    if b:
                        dve.wait_ge(yt_ready, TPC * (b - 1) + t + 1)
                    nc.vector.scalar_tensor_tensor(y[:, t, :], ln[:, b % 2, t, :], rrms[:, b % 2, t:t + 1], rmsw[:, :],
                                                   ALU.mult, ALU.mult).then_inc(y_ready, 1)
                if b < NCH - 1:
                    layer_norm(b + 1)
                for t in range(TPC):
                    cols = slice((b * TPC + t) * P, (b * TPC + t + 1) * P)
                    dve.wait_ge(hi_ready, b * TPC + t + 1)
                    nc.vector.tensor_tensor(yl[:, :, cols], pt[:, t], yh[:, :, cols], ALU.subtract).then_inc(lo_ready, 1)

        @block.gpsimd
        def _(pool):
            def inverse_std(b):
                pool.wait_ge(var_ready, b + 1)
                nc.gpsimd.tensor_tensor(rstd[:, b % 2, :], veps[:, b % 2, :], mhalf[:, :], ALU.pow).then_inc(rstd_ready, 1)

            pool.wait_ge(half_set, 1)
            inverse_std(0)
            for b in range(NCH):
                pool.wait_ge(ssq_ready, TPC * (b + 1))
                nc.gpsimd.tensor_scalar(meps[:, b % 2, :], ssq[:, b % 2, :], 1.0 / D, RMS_EPS, ALU.mult,
                                        ALU.add).then_inc(ms_ready, 1)
                pool.wait_ge(ms_ready, b + 1)
                nc.gpsimd.tensor_tensor(rrms[:, b % 2, :], meps[:, b % 2, :], mhalf[:, :], ALU.pow).then_inc(rrms_ready, 1)
                if b < NCH - 1:
                    inverse_std(b + 1)
                pool.wait_ge(ln_ready, TPC * (b + 1))
                for t in range(TPC):
                    n = b * TPC + t
                    nc.gpsimd.tensor_tensor(xin[:, n, :], xin[:, n, :], ln[:, b % 2, t, :], ALU.add).then_inc(z_ready, 1)

        @block.scalar
        def _(act):
            def squares(b):
                for t in range(TPC):
                    n = b * TPC + t
                    act.wait_ge(ln_ready, n + 1)
                    if n >= 2:
                        act.wait_ge(ssq_ready, n - 1)
                    nc.scalar.activation(sq[:, n % 2, :], ln[:, b % 2, t, :], ACT.Square,
                                         accum_out=ssq[:, b % 2, t:t + 1]).then_inc(ssq_ready, 1)

            squares(0)
            for b in range(NCH):
                for t in range(TPC):
                    n = b * TPC + t
                    act.wait_ge(yt_ready, n + 1)
                    nc.scalar.activation(yh[:, :, n * P:(n + 1) * P], pt[:, t], ACT.Copy).then_inc(hi_ready, 1)
                if b < NCH - 1:
                    squares(b + 1)

        @block.tensor
        def _(pe):
            pe.wait_ge(ident_in, 16)
            for n in range(TT):
                pe.wait_ge(y_ready, n + 1)
                if n >= TPC:
                    pe.wait_ge(lo_ready, n - TPC + 1)
                for k in range(KT):
                    last = nc.tensor.transpose(pt[:, n % TPC, k, :], y[:, n % TPC, k * P:(k + 1) * P], ident[:, :])
                last.then_inc(yt_ready, 1)


UNITS = NCH * HG
KEY_TILES = [TPC * (u // HG + 1) for u in range(UNITS)]
FIRST_STEP = [sum(KEY_TILES[:u]) for u in range(UNITS + 1)]
STEPS = FIRST_STEP[UNITS]
PIECES = STEPS
PV_LAG = 5
RING = 10
RING32 = 8
SBANKS = 3
OUT_LAG = PV_LAG - 2
TURN_LAG = 1
V_LAG = 3
ROPE_LAG = 3
TILES_KEPT = 4
HEAD = 3
MROW_SLOT = (2, 4, 4, 4)
TURN_PARTS = (0, 1, 2, HG, 3)
POOL_STEPS = [i for i in range(STEPS) if (i % 2 if i < FIRST_STEP[13] else i % 5 in (1, 3))]
DVE_STEPS = [i for i in range(STEPS) if i not in POOL_STEPS]
DVE_HEAD, POOL_HEAD = (sum(i < HEAD for i in steps) for steps in (DVE_STEPS, POOL_STEPS))


def step_of(i):
    u = max(w for w in range(UNITS) if FIRST_STEP[w] <= i)
    return u, i - FIRST_STEP[u]


def first_query_tile(c, j):
    return max(0, j - TPC * c)


def score_bank(i):
    return i % SBANKS if i < STEPS - 1 else 1


def bank_before(i):
    return next(p for p in range(i - 1, i - 1 - 2 * SBANKS, -1) if score_bank(p % STEPS) == score_bank(i))


EXP_AHEAD = -min(bank_before(i) for i in range(SBANKS + 1))


def opening():
    idle = [(None, None, [])] * (ROPE_LAG - TURN_LAG)
    out = [(None, ("proj", 0, t), []) for t in range(TPC)] + idle
    out += [(None, ("turn", 0, 0, part), []) for part in TURN_PARTS]
    out += [(None, None, [])]
    out += [(None, ("proj", 0, TPC + i), [(0, 0, i)]) for i in range(KEY_TILES[0])]
    out += [(None, ("mrow", 0, 0) if i == MROW_SLOT[0] else None, [(0, 1, i)]) for i in range(KEY_TILES[1])]
    out += [(None, ("turn", 0, 1, part), []) for part in TURN_PARTS[:-1]]
    return out


def slots():
    jobs = {}
    mrow_slots = [FIRST_STEP[u] + MROW_SLOT[u // HG] for u in range(UNITS)]

    def place(slots, items):
        free = [n for n in slots if n not in mrow_slots and n not in jobs]
        jobs.update({free[i * len(free) // len(items)]: item for i, item in enumerate(items)})

    projections = lambda ahead, c: [("proj", ahead, TPC * c + t) for t in range(TPC)]
    turns = lambda ahead, c, parts: [("turn", ahead, c, part) for part in parts]
    first = FIRST_STEP
    place(range(1, 2), turns(0, 1, TURN_PARTS[-1:]))
    place(range(3, first[4] - ROPE_LAG), projections(0, 2))
    place(range(first[4], first[6]), turns(0, 2, TURN_PARTS))
    place(range(first[6] - 1, first[8] - ROPE_LAG), projections(0, 3))
    place(range(first[8], first[10]), turns(0, 3, TURN_PARTS))
    place(range(first[10], first[12]), projections(1, 0))
    place(range(first[12], first[14] - 4), turns(1, 0, TURN_PARTS))
    place(range(first[14] - 4, first[15] - 4), projections(1, 1))
    place(range(first[15], first[16]), turns(1, 1, TURN_PARTS[:-1]))
    for u in range(UNITS):
        jobs[FIRST_STEP[u] + MROW_SLOT[u // HG]] = ("mrow", *divmod(u + 1, UNITS))
    out = []
    for u in range(UNITS):
        n = KEY_TILES[u]
        ahead, w = divmod(u + 2, UNITS)
        m = KEY_TILES[w]
        for j in range(n):
            pieces = [(ahead, w, i) for i in range(j * m // n, (j + 1) * m // n)]
            out.append((FIRST_STEP[u] + j, jobs.get(FIRST_STEP[u] + j), pieces))
    return out


OPENING = opening()
SLOTS = slots()
JOBS = [job for _, job, _ in SLOTS if job]


def side_work(part):
    return [item for _, job, pieces in part
            for item in [("piece", *p) for p in pieces[:1]] + ([job] if job else []) + [("piece", *p) for p in pieces[1:]]]


OPENING_SIDE = side_work(OPENING)
SLOTS_SIDE = side_work(SLOTS)


def turn_count(c, part):
    return (HG + 1) * c + TURN_PARTS.index(part) + 1


def side_of(part):
    return OPENING_SIDE if part is OPENING else SLOTS_SIDE
OPENING_JOBS = [job for _, job, _ in OPENING if job]
W_SPLIT = {FIRST_STEP[9] + 3 * kt: kt for kt in range(KT)}
TURNS = NCH * (HG + 1)


def slot(part, n):
    return part[n] if 0 <= n < len(part) else (None, None, [])


def attention(nc, w_in_t, w_out_t, attn_dram, yh, yl, ident, consts, cos, sin, wraw, raw):
    w_v = w_in_t.rearrange("g (k p) n -> p g k n", p=P)
    out_v = attn_dram.rearrange("(c t p) (g d) -> p c t g d", p=P, c=NCH, g=GROUPS)
    with ExitStack() as ctx:
        sb = lambda name, shape, dt: ctx.enter_context(nc.sbuf_tensor(name, shape, dt))
        sem = lambda name: ctx.enter_context(nc.semaphore(name))
        ident16, big, mask_kq, mask_qk = (consts[:, i, :] for i in range(4))
        wh = sb("wh", [P, KT, GC], F16)
        wl = sb("wl", [P, KT, GC], F16)
        proj = sb("proj", [P, TILES_KEPT, GC], F32)
        rope_a = sb("rope_a", [P, TILES_KEPT, HG + 1, DH], F32)
        rope_b = sb("rope_b", [P, TILES_KEPT, HG + 1, DH], F32)
        roped = sb("roped", [P, TPC, HG + 1, 2, DH], F32)
        k_hl = sb("k_hl", [P, 2, S], F16)
        k_h1 = sb("k_h1", [P, 2, S], F16)
        v = sb("v", [P, 2, TT, VW], F16)
        q_hh = sb("q_hh", [P, 2, HG, CHUNK], F16)
        q_lm = sb("q_lm", [P, 2, HG, CHUNK], F16)
        mpart = sb("mpart", [P, 2, TPC, NCH], F32)
        mrow = sb("mrow", [P, 2, TPC], F32)
        mpre = sb("mpre", [P, 2, TPC, P], F16)
        p32 = sb("p32", [P, RING32, CHUNK], F32)
        ph = sb("ph", [P, RING, CHUNK], F16)
        pl = sb("pl", [P, RING, CHUNK], F16)
        osb = sb("osb", [P, 2, TPC, VU], F32)
        osum = sb("osum", [P, 2, TPC, DH], F32)
        rden = sb("rden", [P, 2, TPC], F32)
        onorm = sb("onorm", [P, 2, TPC, HG, DH], F32)
        credit = sb("credit", [P, 16], F32)
        ps = ctx.enter_context(nc.psum_tensor("a_ps", [P, 8, 512], F32))
        sbank = lambda i: ps[:, score_bank(i), :]
        side_bank = lambda part, item: ps[:, 3 + side_of(part).index(item) % 3, :]
        obank = ps[:, 6:8, :]
        o_read = obank[:, :, 0:2 * VW].rearrange("p a (t w) -> p a t w", w=VW)[:, :, :, 0:VU]

        w_out_in = sem("w_out_in")
        ones_set = sem("ones_set")
        rows_set = sem("rows_set")
        w_loaded = sem("w_loaded")
        w_high = sem("w_high")
        w_low = sem("w_low")
        misc_ready = sem("misc_ready")
        proj_out = sem("proj_out")
        rope_parts = sem("rope_parts")
        v_high = sem("v_high")
        roped_ready = sem("roped_ready")
        turn_high = sem("turn_high")
        turn_low = sem("turn_low")
        scores_ready = sem("scores_ready")
        maxs_ready = sem("maxs_ready")
        maxs_used = sem("maxs_used")
        m_done = sem("m_done")
        m_high = sem("m_high")
        m_ready = sem("m_ready")
        mrow_ready = sem("mrow_ready")
        exp_done = sem("exp_done")
        low_dve = sem("low_dve")
        low_pool = sem("low_pool")
        pv_done = sem("pv_done")
        o_out = sem("o_out")
        o_sum = sem("o_sum")
        o_rden = sem("o_rden")
        o_norm = sem("o_norm")
        o_stored = [sem(f"o_stored{i}") for i in range(2)]
        block = ctx.enter_context(nc.Block())

        def wait_low(eng, g, i):
            if i in POOL_STEPS:
                eng.wait_ge(low_pool, g * len(POOL_STEPS) + POOL_STEPS.index(i) + 1)
            else:
                eng.wait_ge(low_dve, g * len(DVE_STEPS) + DVE_STEPS.index(i) + 1)

        @block.sync
        def _(sp):
            load_w = lambda g: sp.dma_start(wraw[:, :, :], w_v[:, bass.ds(g, 1), :, :].rearrange("p a k n -> p (a k) n"))\
                .then_inc(w_loaded, 16)
            sp.dma_start(raw.rearrange("p (k n) -> p k n", n=D), w_out_t.rearrange("(k p) n -> p k n", p=P))\
                .then_inc(w_out_in, 16)
            with sp.Fori(0, GROUPS) as g:
                sp.wait_ge(w_low, (g + 1) * KT)
                load_w(g + 1)
                for c in range(NCH):
                    sp.wait_ge(o_norm, g * UNITS + HG * (c + 1) + 2)
                    sp.dma_start(out_v[:, c, :, bass.ds(g, 1), :].rearrange("p t a d -> p t (a d)"),
                                 onorm[:, c % 2].rearrange("p t h d -> p t (h d)")).then_inc(o_stored[c % 2], 16)
            sp.wait_ge(w_loaded, 16 * (GROUPS + 1))
            sp.wait_ge(w_out_in, 16)
            for s in o_stored:
                sp.wait_ge(s, 16 * NCH // 2 * GROUPS + 16)

        @block.tensor
        def _(pe):
            pe.wait_ge(ones_set, 3)
            def group(g, par, part):
                def side_read(kind, ahead, *arg):
                    if kind == "piece":
                        pe.wait_ge(maxs_used, (g + ahead) * PIECES + FIRST_STEP[arg[0]] + arg[1] + 1)
                    elif kind == "proj":
                        pe.wait_ge(proj_out, (g + ahead) * TT + arg[0] + 1)
                    elif kind == "turn":
                        pe.wait_ge(turn_low, (g + ahead) * TURNS + turn_count(*arg))
                    else:
                        pe.wait_ge(mrow_ready, (g + ahead) * UNITS + arg[0] + 1 + 2)

                def take_bank(*item):
                    r = side_of(part).index(item)
                    if r >= 3:
                        side_read(*side_of(part)[r - 3])
                    elif part is SLOTS:
                        side_read("piece", 0, 1, KEY_TILES[1] - 1)
                        side_read("mrow", 0, 0)
                        side_read("turn", 0, 1, TURN_PARTS[-2])
                    return side_bank(part, item)

                def project(ahead, t):
                    if t == 0:
                        pe.wait_ge(w_low, (g + ahead + 1) * KT)
                    bank = take_bank("proj", ahead, t)
                    tok = slice(t * P, (t + 1) * P)
                    passes = [(yh, wh), (yh, wl), (yl, wh)]
                    for kt in range(KT):
                        for n, (a, b) in enumerate(passes):
                            last = nc.tensor.matmul(bank[:, 0:GC], a[:, kt, tok], b[:, kt, :],
                                                    start=(kt == 0 and n == 0), stop=(kt == KT - 1 and n == 2))
                    last.then_inc(misc_ready, 1)

                def turn(ahead, c, e):
                    pe.wait_ge(roped_ready, (g + ahead) * TT + TPC * (c + 1) + TILES_KEPT)
                    bank = take_bank("turn", ahead, c, e)
                    for t in range(TPC):
                        last = nc.tensor.transpose(bank[:, t * P:(t + 1) * P],
                                                   roped[:, t, e].rearrange("p a d -> p (a d)"), ident[:, :])
                    last.then_inc(misc_ready, 1)

                def max_rows(ahead, u):
                    pe.wait_ge(m_ready, (g + ahead) * UNITS + u + 1)
                    bank = take_bank("mrow", ahead, u).bitcast(F16)
                    for t in range(TPC):
                        last = nc.tensor.transpose(bank[:, t * P:(t + 1) * P], mpre[:, u % 2, t, :], ident16)
                    last.then_inc(misc_ready, 1)

                def max_piece(ahead, u, i):
                    c, h = divmod(u, HG)
                    t, kk = divmod(i, c + 1)
                    if h == 0 and i == 0:
                        pe.wait_ge(turn_high, (g + ahead) * TURNS + (HG + 1) * (c + 1))
                        pe.wait_ge(turn_low, (g + ahead) * TURNS + (HG + 1) * (c + 1))
                    bank = take_bank("piece", ahead, u, i)
                    width = CHUNK if kk < c else (t + 1) * P
                    last = nc.tensor.matmul(bank[:, 0:width], q_hh[:, c % 2, h, t * P:(t + 1) * P],
                                            k_hl[:, par ^ ahead, kk * CHUNK:kk * CHUNK + width], start=True, stop=(kk < c))
                    if kk == c:
                        last = nc.tensor.matmul(bank[:, width - P:width], big, mask_qk, start=False, stop=True)
                    last.then_inc(maxs_ready, 1)

                def scores(i, ahead=0):
                    gg, side = g + ahead, par ^ ahead
                    u, j = step_of(i)
                    c, h = divmod(u, HG)
                    if j == 0:
                        pe.wait_ge(mrow_ready, gg * UNITS + u + 1 + 2)
                    pe.wait_ge(exp_done, gg * STEPS + bank_before(i) + 1 + EXP_AHEAD)
                    r = first_query_tile(c, j)
                    diag = j >= TPC * c
                    keys = slice(j * P, (j + 1) * P)
                    out = sbank(i)[:, r * P:CHUNK]
                    nc.tensor.matmul(out, k_hl[:, side, keys], q_hh[:, c % 2, h, r * P:CHUNK], start=True, stop=False)
                    last = nc.tensor.matmul(out, k_h1[:, side, keys], q_lm[:, c % 2, h, r * P:CHUNK],
                                            start=False, stop=not diag)
                    if diag:
                        last = nc.tensor.matmul(sbank(i)[:, r * P:(r + 1) * P], big, mask_kq, start=False, stop=True)
                    last.then_inc(scores_ready, 1)

                def values(i):
                    u, j = step_of(i)
                    c = u // HG
                    if j == 0:
                        pe.wait_ge(o_out, g * UNITS + u + 1)
                    pe.wait_ge(exp_done, g * STEPS + i + 1 + EXP_AHEAD)
                    wait_low(pe, g, i)
                    for t in range(first_query_tile(c, j), TPC):
                        o = obank[:, t // 2, (t % 2) * VW:(t % 2) * VW + VU]
                        nc.tensor.matmul(o, ph[:, i % RING, t * P:(t + 1) * P], v[:, par, j, 0:VU],
                                         start=(j == 0 and t % 2 == 0), stop=False, skip_group_check=True)
                        last = nc.tensor.matmul(o[:, 0:DH + 1], pl[:, i % RING, t * P:(t + 1) * P], v[:, par, j, 0:DH + 1],
                                                start=False, stop=(j == TPC * c + t), skip_group_check=True)
                    last.then_inc(pv_done, 1)

                for step, job, pieces in part:
                    if step is not None and step >= HEAD:
                        scores(step)
                    for piece in pieces[:1]:
                        max_piece(*piece)
                    used = step - PV_LAG if step is not None else -1
                    starts_unit = used in FIRST_STEP
                    if used >= 0 and not starts_unit:
                        values(used)
                    if job:
                        {"proj": project, "turn": turn, "mrow": max_rows}[job[0]](*job[1:])
                    for piece in pieces[1:]:
                        max_piece(*piece)
                    if starts_unit:
                        values(used)
                if part is SLOTS:
                    for i in range(STEPS - PV_LAG, STEPS):
                        if i >= STEPS - HEAD:
                            scores(i - (STEPS - HEAD), ahead=1)
                        values(i)
                else:
                    pe.wait_ge(rows_set, 2)
                    for i in range(HEAD):
                        scores(i)

            group(0, 0, OPENING)
            with pe.Fori(0, GROUPS // 2) as pair:
                for par in range(2):
                    group(pair * 2 + par, par, SLOTS)

        @block.scalar
        def _(act):
            act.wait_ge(ones_set, 3)
            def group(g, par, part):
                jobs_before = 0 if part is OPENING else len(OPENING_JOBS) + g * len(JOBS)

                def weights_high(ahead, kt):
                    if kt == 0:
                        act.wait_ge(w_loaded, (g + ahead + 1) * 16)
                    nc.scalar.activation(wh[:, kt, :], wraw[:, kt, :], ACT.Copy, scale=W_SCALE).then_inc(w_high, 1)

                def exps(i, ahead=0):
                    gg = g + ahead
                    u, j = step_of(i)
                    r = first_query_tile(u // HG, j)
                    act.wait_ge(scores_ready, gg * STEPS + i + 1)
                    if i >= RING or ahead:
                        act.wait_ge(pv_done, gg * STEPS + i - RING + 1)
                    if i >= RING32 or ahead:
                        wait_low(act, g, (i - RING32) % STEPS)
                    s = sbank(i)[:, r * P:CHUNK]
                    nc.scalar.activation(p32[:, i % RING32, r * P:CHUNK], s, ACT.Exp, scale=SCALE)
                    nc.scalar.activation(ph[:, i % RING, r * P:CHUNK], s, ACT.Exp, scale=SCALE).then_inc(exp_done, 1)

                def job_out(k, kind, ahead, *arg):
                    act.wait_ge(misc_ready, jobs_before + k + 1)
                    side = par ^ ahead
                    bank = side_bank(part, (kind, ahead, *arg))
                    if kind == "proj":
                        t, = arg
                        act.wait_ge(roped_ready, (g + ahead) * TT + t + 1)
                        nc.scalar.activation(proj[:, t % TILES_KEPT, :], bank[:, 0:GC], ACT.Copy,
                                             scale=1.0 / W_SCALE).then_inc(proj_out, 1)
                    elif kind == "turn":
                        c, e = arg
                        if e < HG:
                            nc.scalar.activation(q_hh[:, c % 2, e, :], bank, ACT.Copy).then_inc(turn_high, 1)
                        else:
                            cols = slice(c * CHUNK, (c + 1) * CHUNK)
                            nc.scalar.activation(k_h1[0:DH, side, cols], bank[0:DH, :], ACT.Copy)
                            nc.scalar.activation(k_hl[:, side, cols], bank, ACT.Copy).then_inc(turn_high, 1)
                    else:
                        c, h = divmod(arg[0], HG)
                        nc.scalar.activation(q_lm[DH:P, c % 2, h, :], bank.bitcast(F16)[DH:P, 0:CHUNK], ACT.Copy)\
                            .then_inc(mrow_ready, 1)

                def unit_out(u):
                    act.wait_ge(pv_done, g * STEPS + FIRST_STEP[u + 1])
                    act.wait_ge(o_norm, g * UNITS + u + 1)
                    nc.scalar.activation(osb[:, u % 2].rearrange("p (a t) w -> p a t w", a=2), o_read,
                                         ACT.Copy).then_inc(o_out, 1)

                if part is OPENING:
                    for kt in range(KT):
                        weights_high(0, kt)
                k = 0
                for n in range(len(part) + 1):
                    step = slot(part, n)[0]
                    if job := slot(part, n - 1)[1]:
                        job_out(k, *job)
                        k += 1
                    if step is not None:
                        if step >= HEAD:
                            exps(step)
                        if step in W_SPLIT:
                            weights_high(1, W_SPLIT[step])
                    if step is not None and step - OUT_LAG in FIRST_STEP[1:]:
                        unit_out(FIRST_STEP.index(step - OUT_LAG) - 1)
                for i in range(HEAD):
                    exps(i, ahead=int(part is SLOTS))
                if part is SLOTS:
                    unit_out(UNITS - 1)

            group(0, 0, OPENING)
            with act.Fori(0, GROUPS // 2) as pair:
                for par in range(2):
                    group(pair * 2 + par, par, SLOTS)

        @block.vector
        def _(dve):
            nc.vector.memset(v[:, :, :, DH:DH + 1], 1.0).then_inc(ones_set, 1)
            nc.vector.memset(mpre[:, :, :, :], 0.0).then_inc(ones_set, 1)
            for n, (s, ahead) in enumerate(((roped_ready, TILES_KEPT), (mrow_ready, 2), (exp_done, EXP_AHEAD),
                                             (o_out, 1), (o_norm, 2), (o_stored[0], 16), (o_stored[1], 16), (w_loaded, 16))):
                nc.vector.memset(credit[:, n:n + 1], 0.0).then_inc(s, ahead)
            nc.vector.memset(credit[:, 15:16], 0.0).then_inc(ones_set, 1)
            def group(g, par, part):
                def weights_low(ahead, kt):
                    dve.wait_ge(w_high, (g + ahead) * KT + kt + 1)
                    nc.vector.scalar_tensor_tensor(wl[:, kt, :], wraw[:, kt, :], W_SCALE, wh[:, kt, :], ALU.mult,
                                                   ALU.subtract).then_inc(w_low, 1)

                def low_part(i, ahead=0):
                    u, j = step_of(i)
                    r = first_query_tile(u // HG, j)
                    cols = slice(r * P, CHUNK)
                    dve.wait_ge(exp_done, (g + ahead) * STEPS + i + 1 + EXP_AHEAD)
                    nc.vector.tensor_tensor(pl[:, i % RING, cols], p32[:, i % RING32, cols], ph[:, i % RING, cols],
                                            ALU.subtract).then_inc(low_dve, 1)

                def reduce_piece(ahead, u, i):
                    gg, c, n = g + ahead, u // HG, FIRST_STEP[u] + i
                    t, kk = divmod(i, c + 1)
                    width = CHUNK if kk < c else (t + 1) * P
                    dve.wait_ge(maxs_ready, gg * PIECES + n + 1)
                    nc.vector.reduce_max(mpart[:, u % 2, t, kk:kk + 1], side_bank(part, ("piece", ahead, u, i))[:, 0:width], AX.X)\
                        .then_inc(maxs_used, 1)
                    if i < KEY_TILES[u] - 1:
                        return
                    dve.wait_ge(maxs_used, gg * PIECES + n + 1)
                    nc.vector.reduce_max(mrow[:, u % 2, :], mpart[:, u % 2, :, 0:c + 1], AX.X).then_inc(m_done, 1)
                    dve.wait_ge(m_done, gg * UNITS + u + 1)
                    dve.wait_ge(mrow_ready, gg * UNITS + u + 1)
                    high, low = mpre[:, u % 2, :, DH:DH + 1], mpre[:, u % 2, :, DH + 1:DH + 2]
                    m = mrow[:, u % 2, :].unsqueeze(2)
                    nc.vector.tensor_scalar(high, m, -1.0 / M_SCALE, None, ALU.mult).then_inc(m_high, 1)
                    dve.wait_ge(m_high, gg * UNITS + u + 1)
                    nc.vector.scalar_tensor_tensor(low, m, -1.0 / M_SCALE, high, ALU.mult,
                                                   ALU.subtract).then_inc(m_ready, 1)

                def split_v(ahead, t):
                    gg, side = g + ahead, par ^ ahead
                    vp = proj[:, t % TILES_KEPT, (HG + 1) * DH:GC]
                    dve.wait_ge(proj_out, gg * TT + t + 1)
                    nc.vector.tensor_copy(v[:, side, t, 0:DH], vp).then_inc(v_high, 1)
                    dve.wait_ge(v_high, gg * TT + t + 1)
                    nc.vector.tensor_tensor(v[:, side, t, DH + 1:VU], vp, v[:, side, t, 0:DH], ALU.subtract)

                def turn_low_part(ahead, c, e):
                    side, bank = par ^ ahead, side_bank(part, ("turn", ahead, c, e))
                    dve.wait_ge(turn_high, (g + ahead) * TURNS + turn_count(c, e))
                    if e < HG:
                        nc.vector.tensor_tensor(q_lm[0:DH, c % 2, e, :], bank[0:DH, :],
                                                q_hh[0:DH, c % 2, e, :], ALU.subtract).then_inc(turn_low, 1)
                    else:
                        cols = slice(c * CHUNK, (c + 1) * CHUNK)
                        nc.vector.tensor_tensor(k_hl[DH:P, side, cols], bank[DH:P, :], k_hl[DH:P, side, cols],
                                                ALU.subtract).then_inc(turn_low, 1)

                def unit_reciprocal(u):
                    dve.wait_ge(o_out, g * UNITS + u + 1 + 1)
                    nc.vector.reciprocal(rden[:, u % 2, :].unsqueeze(2), osb[:, u % 2, :, DH:DH + 1])\
                        .then_inc(o_rden, 1)

                if part is OPENING:
                    for kt in range(KT):
                        weights_low(0, kt)
                for n in range(len(part) + V_LAG):
                    for piece in slot(part, n - 1)[2]:
                        reduce_piece(*piece)
                    step = slot(part, n - 1)[0]
                    if step is not None:
                        if step in W_SPLIT:
                            weights_low(1, W_SPLIT[step])
                    if slot(part, n - 3)[0] in DVE_STEPS[DVE_HEAD:]:
                        low_part(slot(part, n - 3)[0])
                    if (job := slot(part, n - TURN_LAG)[1]) and job[0] == "turn":
                        turn_low_part(*job[1:])
                    if (job := slot(part, n - V_LAG)[1]) and job[0] == "proj":
                        split_v(*job[1:])
                    step = slot(part, n - 2)[0]
                    if step is not None and step - OUT_LAG in FIRST_STEP[1:]:
                        unit_reciprocal(FIRST_STEP.index(step - OUT_LAG) - 1)
                for i in DVE_STEPS[:DVE_HEAD]:
                    low_part(i, ahead=int(part is SLOTS))
                if part is SLOTS:
                    unit_reciprocal(UNITS - 1)

            group(0, 0, OPENING)
            with dve.Fori(0, GROUPS // 2) as pair:
                for par in range(2):
                    group(pair * 2 + par, par, SLOTS)

        @block.gpsimd
        def _(pool):
            nc.gpsimd.memset(k_h1[DH:P, :, :], 0.0).then_inc(rows_set, 1)
            pool.wait_ge(rows_set, 1)
            nc.gpsimd.memset(k_h1[DH:DH + 2, :, :], M_SCALE).then_inc(rows_set, 1)
            pool.wait_ge(rows_set, 2)
            pool.wait_ge(ones_set, 3)
            def group(g, par, part):
                def low_part(i, ahead=0):
                    u, j = step_of(i)
                    r = first_query_tile(u // HG, j)
                    cols = slice(r * P, CHUNK)
                    pool.wait_ge(exp_done, (g + ahead) * STEPS + i + 1 + EXP_AHEAD)
                    nc.gpsimd.tensor_tensor(pl[:, i % RING, cols], p32[:, i % RING32, cols], ph[:, i % RING, cols],
                                            ALU.subtract).then_inc(low_pool, 1)

                def rope(ahead, t):
                    b, half = t % TILES_KEPT, DH // 2
                    heads = proj[:, b, 0:(HG + 1) * DH].rearrange("p (h d) -> p h d", d=DH)
                    spread = lambda a, w: a.unsqueeze(1).broadcast_to([P, HG + 1, w])
                    pool.wait_ge(proj_out, (g + ahead) * TT + t + 1)
                    pool.wait_ge(roped_ready, (g + ahead) * TT + t + 1)
                    nc.gpsimd.tensor_tensor(rope_a[:, b], heads, spread(cos[:, t, :], DH), ALU.mult)
                    nc.gpsimd.tensor_tensor(rope_b[:, b, :, 0:half], heads[:, :, half:DH],
                                            spread(sin[:, t, 0:half], half), ALU.mult)
                    nc.gpsimd.tensor_tensor(rope_b[:, b, :, half:DH], heads[:, :, 0:half],
                                            spread(sin[:, t, half:DH], half), ALU.mult).then_inc(rope_parts, 1)

                def rope_sum(ahead, t):
                    if t % TPC == 0 and (t or ahead):
                        pool.wait_ge(turn_low, (g + ahead) * TURNS + (HG + 1) * (t // TPC))
                    pool.wait_ge(rope_parts, (g + ahead) * TT + t + 1)
                    twice = lambda a: a[:, t % TILES_KEPT].unsqueeze(2).broadcast_to([P, HG + 1, 2, DH])
                    nc.gpsimd.tensor_tensor(roped[:, t % TPC], twice(rope_a), twice(rope_b), ALU.add)\
                        .then_inc(roped_ready, 1)

                def unit_normalise(u):
                    c, h = divmod(u, HG)
                    pool.wait_ge(o_out, g * UNITS + u + 1 + 1)
                    nc.gpsimd.tensor_tensor(osum[:, u % 2], osb[:, u % 2, :, 0:DH], osb[:, u % 2, :, DH + 1:VU],
                                            ALU.add).then_inc(o_sum, 1)
                    pool.wait_ge(o_sum, g * UNITS + u + 1)
                    pool.wait_ge(o_rden, g * UNITS + u + 1)
                    if h == 0:
                        pool.wait_ge(o_stored[c % 2], g * (16 * NCH // 2) + 16 * (c // 2 + 1))
                    nc.gpsimd.tensor_tensor(onorm[:, c % 2, :, h, :], osum[:, u % 2],
                                            rden[:, u % 2, :].unsqueeze(2).broadcast_to([P, TPC, DH]),
                                            ALU.mult).then_inc(o_norm, 1)

                for n in range(len(part) + 1):
                    if (job := slot(part, n - 1)[1]) and job[0] == "proj":
                        rope(*job[1:])
                    step = slot(part, n - 1)[0]
                    if step is not None:
                        if step in POOL_STEPS[POOL_HEAD:]:
                            low_part(step)
                        if step - OUT_LAG in FIRST_STEP[1:]:
                            unit_normalise(FIRST_STEP.index(step - OUT_LAG) - 1)
                    if (job := slot(part, n - 1)[1]) and job[0] == "proj":
                        rope_sum(*job[1:])
                for i in POOL_STEPS[:POOL_HEAD]:
                    low_part(i, ahead=int(part is SLOTS))
                if part is SLOTS:
                    unit_normalise(UNITS - 1)

            group(0, 0, OPENING)
            with pool.Fori(0, GROUPS // 2) as pair:
                for par in range(2):
                    group(pair * 2 + par, par, SLOTS)


def output_projection(nc, raw, ffn_t, ident, attn_dram, resid_dram, tern, scale, x2, xh, xl):
    a_v = attn_dram.rearrange("(n p) (q c) -> p n q c", p=P, q=NQ)
    r_v = resid_dram.rearrange("(n p) d -> p n d", p=P)
    f_v = ffn_t.rearrange("m p n -> p m n")
    with ExitStack() as ctx:
        sb = lambda name, shape, dt: ctx.enter_context(nc.sbuf_tensor(name, shape, dt))
        sem = lambda name: ctx.enter_context(nc.semaphore(name))
        ones = sb("p_ones", [P, P], F32)
        mhalf = sb("p_mhalf", [P, 1], F32)
        wh = sb("p_wh", [P, CT, D], F16)
        wl = sb("p_wl", [P, CT, D], F16)
        att = sb("p_att", [P, NQ, QC], F32)
        ath = sb("p_ath", [P, 2, CT, P], F16)
        atl = sb("p_atl", [P, 2, CT, P], F16)
        stats = sb("p_stats", [P, 6], F32)
        mv = sb("p_mv", [P, 2], F32)
        veps = sb("p_veps", [P, 1], F32)
        rstd = sb("p_rstd", [P, 1], F32)
        ln = sb("p_ln", [P, D], F32)
        sums = sb("p_abs_sums", [P, 3, NQ], F32)
        total = sb("p_abs_total", [P, 3], F32)
        half = sb("p_half", [P, 3, 2], F32)
        below = sb("p_below", [P, 2, QN // 2], F16)
        credit = sb("p_credit", [P, 3], F32)
        ps = ctx.enter_context(nc.psum_tensor("p_ps", [P, 8, 512], F32))
        tbank = lambda q: ps[:, q, :]
        ybank = lambda i: ps[:, 4 + i % 2, :]
        lbank = ps[:, 6, :]
        abank = ps[:, 7, :]
        by_tile = lambda bank: bank.rearrange("p (k n) -> p k n", k=4)
        raw_q = lambda q: raw[:, q * QN:(q + 1) * QN]
        halves = lambda r: slice(r * QN // 2, (r + 1) * QN // 2)
        raw_h = lambda r: raw[:, halves(r)]
        tern_h = lambda c, r: tern[:, bass.ds(c, 1), halves(r)].rearrange("p a n -> p (a n)")

        ones_set = sem("p_ones_set")
        half_set = sem("p_half_set")
        raw_in = [sem(f"p_raw_in{q}") for q in range(NQ)]
        raw_used = sem("p_raw_used")
        w_high = sem("p_w_high")
        z_in = sem("p_z_in")
        att_in = [sem(f"p_att_in{q}") for q in range(NQ)]
        turned = sem("p_turned")
        t_high = sem("p_t_high")
        t_low = sem("p_t_low")
        y_ready = sem("p_y_ready")
        x2_ready = sem("p_x2_ready")
        stat = sem("p_stat")
        aggr = sem("p_aggr")
        var_ready = sem("p_var_ready")
        rstd_ready = sem("p_rstd_ready")
        ln_ready = sem("p_ln_ready")
        ln_turned = sem("p_ln_turned")
        ln_high = sem("p_ln_high")
        ln_low = sem("p_ln_low")
        summed = sem("p_abs_summed")
        totalled = sem("p_abs_totalled")
        spread = sem("p_abs_spread")
        scaled = sem("p_scale_ready")
        tern_ready = sem("p_tern_ready")
        block = ctx.enter_context(nc.Block())

        COMPARED = [[[], [0], [1, 2], [3]], [[4], [5], [6], [7]]]

        def chunks(eng, steps):
            with eng.Fori(0, NCH - 2) as c:
                steps(c, True, True, True)
            steps(NCH - 2, True, False, True)
            steps(NCH - 1, False, False, False)

        @block.sync
        def _(sp):
            def load_att(n, q, wait=True):
                if wait:
                    sp.wait_ge(turned, NQ * (n - 1) + q + 1)
                sp.dma_start(att[:, q, :], a_v[:, bass.ds(n, 1), q, :].rearrange("p a c -> p (a c)"))\
                    .then_inc(att_in[q], 16)

            def load_z(c):
                tiles = bass.ds(c * TPC, TPC)
                sp.dma_start(x2[:, tiles, :], r_v[:, tiles, :]).then_inc(z_in, 16)

            def load_raw(m, q):
                sp.wait_ge(raw_used, 2 * NQ * m + 2 * q + 2)
                sp.dma_start(raw_q(q), f_v[:, bass.ds(m, 1), q * QN:(q + 1) * QN].rearrange("p a n -> p (a n)"))\
                    .then_inc(raw_in[q], 16)

            for q in range(NQ):
                load_att(0, q, wait=False)
            for q in range(NQ):
                load_att(1, q)
            load_z(0)
            for q in range(NQ):
                load_att(2, q)
            for q in range(NQ // 2):
                load_raw(0, q)

            def steps(c, quantise, load_next, full):
                for t in range(TPC):
                    if full or t < TPC - 3:
                        for q in range(NQ):
                            load_att(c * TPC + t + 3, q)
                    if quantise and t == 0:
                        load_raw(c, 2)
                        load_raw(c, 3)
                    if full and t == 1:
                        load_z(c + 1)
                    if load_next and t == 2:
                        load_raw(c + 1, 0)
                        load_raw(c + 1, 1)

            chunks(sp, steps)

        @block.tensor
        def _(pe):
            def turn(n, q, free=True):
                pe.wait_ge(att_in[q], 16 * n + 16)
                if free:
                    pe.wait_ge(t_low, NQ * (n - 1) + q + 1)
                for k in range(4):
                    last = nc.tensor.transpose(tbank(q)[:, k * P:(k + 1) * P], att[:, q, k * P:(k + 1) * P], ident[:, :])
                last.then_inc(turned, 1)

            def project(n, b, q):
                pe.wait_ge(t_low, NQ * n + q + 1)
                for k in range(4 * q, 4 * q + 4):
                    for j, (a, w) in enumerate([(ath, wh), (ath, wl), (atl, wh)]):
                        last = nc.tensor.matmul(ybank(b), a[:, b, k, :], w[:, k, :], start=(k == 0 and j == 0),
                                                stop=(k == CT - 1 and j == 2))
                if q == NQ - 1:
                    last.then_inc(y_ready, 1)

            pe.wait_ge(ones_set, 1)
            for q in range(NQ):
                turn(0, q, free=False)
            for q in range(NQ):
                pe.wait_ge(raw_used, 2 * q + 2)
                project(0, 0, q)
                turn(1, q)

            def steps(c, quantise, load_next, full):
                for t in range(TPC):
                    i = c * TPC + t
                    for q in range(NQ):
                        if full or t < TPC - 1:
                            project(i + 1, (t + 1) % 2, q)
                        if full or t < TPC - 2:
                            turn(i + 2, q)
                        if q == 1:
                            if quantise and t == 2:
                                pe.wait_ge(totalled, c + 1)
                                nc.tensor.matmul(abank[:, 0:1], ones[:, :], total[:, bass.ds(c, 1)], start=True,
                                                 stop=True).then_inc(spread, 1)
                            pe.wait_ge(ln_ready, i + 1)
                            pe.wait_ge(ln_low, i + 1)
                            for k in range(KT):
                                last = nc.tensor.transpose(lbank[:, k * P:(k + 1) * P], ln[:, k * P:(k + 1) * P],
                                                           ident[:, :])
                            last.then_inc(ln_turned, 1)

            chunks(pe, steps)

        @block.scalar
        def _(act):
            def high(n, b, q):
                act.wait_ge(turned, NQ * n + q + 1)
                nc.scalar.activation(ath[:, b, 4 * q:4 * q + 4, :], by_tile(tbank(q)), ACT.Copy).then_inc(t_high, 1)

            for q in range(NQ):
                nc.scalar.activation(wh[:, 4 * q:4 * q + 4, :], by_tile(raw_q(q)), ACT.Copy,
                                     scale=W_SCALE).then_inc(w_high, 1)
                high(0, 0, q)
            for q in range(NQ):
                high(1, 1, q)

            def steps(c, quantise, load_next, full):
                for t in range(TPC):
                    i = c * TPC + t
                    for q in range(NQ):
                        if full or t < TPC - 2:
                            act.wait_ge(y_ready, i + 1)
                            high(i + 2, t % 2, q)
                        if q == 1:
                            act.wait_ge(ln_turned, i + 1)
                            nc.scalar.activation(xh[:, :, bass.ds(i * P, P)], by_tile(lbank), ACT.Copy).then_inc(ln_high, 1)
                    if quantise and t < 2:
                        for q in (2 * t, 2 * t + 1):
                            act.wait_ge(raw_in[q], 16 * c + 16)
                            nc.scalar.activation(tern[:, bass.ds(c, 1), q * QN:(q + 1) * QN]
                                                 .rearrange("p a n -> p (a n)"), raw_q(q), ACT.Abs,
                                                 accum_out=sums[:, bass.ds(c, 1), q:q + 1]
                                                 .rearrange("p a n -> p (a n)")).then_inc(summed, 1)

            chunks(act, steps)

        @block.vector
        def _(dve):
            nc.vector.memset(mhalf[:, :], -0.5).then_inc(half_set, 1)
            nc.vector.memset(ones[:, :], 1.0).then_inc(ones_set, 1)
            nc.vector.memset(credit[:, 0:1], 0.0).then_inc(ln_low, 1)
            nc.vector.memset(credit[:, 2:3], 0.0).then_inc(tern_ready, 2)

            def low(n, b, q):
                dve.wait_ge(t_high, NQ * n + q + 1)
                out = (slice(None), b, slice(4 * q, 4 * q + 4), slice(None))
                nc.vector.tensor_tensor(atl[out], by_tile(tbank(q)), ath[out], ALU.subtract).then_inc(t_low, 1)

            for q in range(NQ):
                dve.wait_ge(w_high, q + 1)
                nc.vector.scalar_tensor_tensor(wl[:, 4 * q:4 * q + 4, :], by_tile(raw_q(q)), W_SCALE,
                                               wh[:, 4 * q:4 * q + 4, :], ALU.mult, ALU.subtract).then_inc(raw_used, 2)
                low(0, 0, q)
            for q in range(NQ):
                low(1, 1, q)
            dve.wait_ge(z_in, 16)

            def layer_norm(i, b):
                tile = x2[:, bass.ds(i, 1), :].rearrange("p a d -> p (a d)")
                dve.wait_ge(y_ready, i + 1)
                nc.vector.scalar_tensor_tensor(tile, ybank(b), 1.0 / W_SCALE, tile, ALU.mult, ALU.add)\
                    .then_inc(x2_ready, 1)
                dve.wait_ge(x2_ready, i + 1)
                nc.vector.memset(credit[:, 1:2], 0.0)
                nc.vector.bn_stats(stats[:, :], tile).then_inc(stat, 1)
                dve.wait_ge(stat, i + 1)
                nc.vector.memset(credit[:, 1:2], 0.0)
                nc.vector.bn_aggr(mv[:, :], stats[:, :]).then_inc(aggr, 1)
                dve.wait_ge(aggr, i + 1)
                nc.vector.tensor_scalar(veps[:, :], mv[:, 1:2], LN_EPS, None, ALU.add).then_inc(var_ready, 1)
                dve.wait_ge(rstd_ready, i + 1)
                nc.vector.tensor_scalar(ln[:, :], tile, mv[:, 0:1], rstd[:, :], ALU.subtract,
                                        ALU.mult).then_inc(ln_ready, 1)

            def tern_scale(c):
                m = bass.ds(c, 1)
                dve.wait_ge(spread, c + 1)
                nc.vector.tensor_scalar(scale[:, m], abank[:, 0:1], 1.0 / (D * E), Q_EPS,
                                        ALU.mult, ALU.add).then_inc(scaled, 1)
                dve.wait_ge(scaled, 3 * c + 1)
                for side, sign in enumerate((0.5, -0.5)):
                    nc.vector.tensor_scalar(half[:, m, side:side + 1].rearrange("p a n -> p (a n)"), scale[:, m],
                                            sign, None, ALU.mult).then_inc(scaled, 1)
                dve.wait_ge(scaled, 3 * c + 3)

            def compare(c, r):
                n = 2 * NQ * c + r
                limit = lambda side: half[:, bass.ds(c, 1), side:side + 1].rearrange("p a n -> p (a n)")
                dve.wait_ge(tern_ready, n + 1)
                nc.vector.tensor_scalar(below[:, r % 2, :], raw_h(r), limit(1), None, ALU.is_lt)
                compared = nc.vector.tensor_scalar(tern_h(c, r), raw_h(r), limit(0), None, ALU.is_gt)
                compared.then_inc(raw_used, 1)

            def steps(c, quantise, load_next, full):
                m = bass.ds(c, 1)
                for t in range(TPC):
                    i = c * TPC + t
                    layer_norm(i, t % 2)
                    for q in range(NQ):
                        if full or t < TPC - 2:
                            low(i + 2, t % 2, q)
                        if q == 1:
                            dve.wait_ge(ln_high, i + 1)
                            cols = bass.ds(i * P, P)
                            nc.vector.tensor_tensor(xl[:, :, cols], by_tile(lbank), xh[:, :, cols],
                                                    ALU.subtract).then_inc(ln_low, 1)
                        if quantise and t == 2 and q == 0:
                            dve.wait_ge(summed, NQ * c + NQ)
                            nc.vector.reduce_sum(total[:, m], sums[:, m, :].rearrange("p a n -> p (a n)"), AX.X)\
                                .then_inc(totalled, 1)
                        if quantise and t == 2 and q == 1:
                            tern_scale(c)
                        if quantise and t >= 2:
                            for r in COMPARED[t - 2][q]:
                                compare(c, r)
                if full:
                    dve.wait_ge(z_in, 16 * c + 32)

            chunks(dve, steps)

        @block.gpsimd
        def _(pool):
            pool.wait_ge(half_set, 1)

            def steps(c, quantise, load_next, full):
                m = bass.ds(c, 1)
                for t in range(TPC):
                    pool.wait_ge(var_ready, c * TPC + t + 1)
                    nc.gpsimd.tensor_tensor(rstd[:, :], veps[:, :], mhalf[:, :], ALU.pow).then_inc(rstd_ready, 1)
                    if quantise and t >= 2:
                        for r in range(NQ * (t - 2), NQ * (t - 1)):
                            pool.wait_ge(raw_used, 2 * NQ * (c + 1) + r + 1)
                            nc.gpsimd.tensor_tensor(tern_h(c, r), tern_h(c, r), below[:, r % 2, :], ALU.subtract)                                .then_inc(tern_ready, 1)

            chunks(pool, steps)


def feed_forward(nc, tern, scale, x2, xh, xl, out):
    up = tern[:, 0, :].rearrange("p (k n) -> p k n", k=KT)
    gate = tern[:, 1, :].rearrange("p (k n) -> p k n", k=KT)
    down = tern[:, 2, :].rearrange("p (k n) -> p k n", k=ET)
    o_v = out[0].rearrange("(n p) d -> p n d", p=P)
    with ExitStack() as ctx:
        sb = lambda name, shape, dt: ctx.enter_context(nc.sbuf_tensor(name, shape, dt))
        sem = lambda name: ctx.enter_context(nc.semaphore(name))
        credit = sb("f_credit", [P, 4], F32)
        sgd = sb("f_sgd", [P, 1], F32)
        silu = sb("f_silu", [P, 2, CHUNK], F32)
        hid = sb("f_hid", [P, 2, CHUNK], F32)
        hh = sb("f_hh", [P, ET, CHUNK], F16)
        hl = sb("f_hl", [P, ET, CHUNK], F16)
        ps = ctx.enter_context(nc.psum_tensor("f_ps", [P, 8, 512], F32))
        ubank = lambda e: ps[:, e % 2, :]
        gbank = lambda e: ps[:, 2 + e % 2, :]
        dbank = lambda t: ps[:, 4 + t % 2, :]
        sgd_ready = sem("f_sgd_ready")
        up_ready = sem("f_up_ready")
        gate_ready = sem("f_gate_ready")
        silu_ready = sem("f_silu_ready")
        hid_ready = sem("f_hid_ready")
        h_high = sem("f_h_high")
        h_low = sem("f_h_low")
        down_ready = sem("f_down_ready")
        res_ready = sem("f_res_ready")
        res_out = sem("f_res_out")
        block = ctx.enter_context(nc.Block())

        @block.sync
        def _(sp):
            with sp.Fori(0, TT) as i:
                sp.wait_ge(res_ready, i + 3)
                sp.dma_start(o_v[:, bass.ds(i, 1), :], x2[:, bass.ds(i, 1), :]).then_inc(res_out, 16)
            sp.wait_ge(res_out, 16 * TT)

        @block.tensor
        def _(pe):
            def product(bank, w, c, e):
                for k in range(KT):
                    for x in (xh, xl):
                        last = nc.tensor.matmul(bank, w[:, k, e * P:(e + 1) * P], x[:, k, bass.ds(c * CHUNK, CHUNK)],
                                                start=(k == 0 and x is xh), stop=(k == KT - 1 and x is xl))
                return last

            def up_and_gate(c, e):
                pe.wait_ge(silu_ready, c * ET + e + 1)
                product(ubank(e), up, c, e).then_inc(up_ready, 1)
                pe.wait_ge(hid_ready, c * ET + e + 1)
                product(gbank(e), gate, c, e).then_inc(gate_ready, 1)

            def chunk(c, full):
                for e in range(1, ET):
                    up_and_gate(c, e)
                if full:
                    up_and_gate(c + 1, 0)
                pe.wait_ge(h_low, c * ET + ET + 2)
                for t in range(TPC):
                    pe.wait_ge(res_ready, c * TPC + t + 1)
                    for e in range(ET):
                        for h in (hh, hl):
                            last = nc.tensor.matmul(dbank(t), h[:, e, t * P:(t + 1) * P], down[:, e, :],
                                                    start=(e == 0 and h is hh), stop=(e == ET - 1 and h is hl))
                    last.then_inc(down_ready, 1)

            up_and_gate(0, 0)
            with pe.Fori(0, NCH - 1) as c:
                chunk(c, True)
            chunk(NCH - 1, False)

        @block.scalar
        def _(act):
            with act.Fori(0, NCH) as c:
                for e in range(ET):
                    n = c * ET + e
                    act.wait_ge(up_ready, n + 1)
                    act.wait_ge(hid_ready, n + 1)
                    nc.scalar.activation(silu[:, e % 2, :], ubank(e), ACT.Silu, scale=scale[:, 0:1])\
                        .then_inc(silu_ready, 1)

        @block.vector
        def _(dve):
            for n, s in enumerate((silu_ready, hid_ready, h_low, res_ready)):
                nc.vector.memset(credit[:, n:n + 1], 0.0).then_inc(s, 2)
            nc.vector.tensor_tensor(sgd[:, :], scale[:, 1:2], scale[:, 2:3], ALU.mult).then_inc(sgd_ready, 1)

            def hidden(c, e):
                n = c * ET + e
                dve.wait_ge(silu_ready, n + 3)
                dve.wait_ge(gate_ready, n + 1)
                dve.wait_ge(h_low, n + 1)
                nc.vector.tensor_tensor(hid[:, e % 2, :], silu[:, e % 2, :], gbank(e), ALU.mult).then_inc(hid_ready, 1)

            def high(c, e):
                dve.wait_ge(hid_ready, c * ET + e + 3)
                nc.vector.tensor_copy(hh[:, e, :], hid[:, e % 2, :]).then_inc(h_high, 1)

            def result(c, t):
                i = c * TPC + t
                tile = x2[:, bass.ds(i, 1), :].rearrange("p a d -> p (a d)")
                dve.wait_ge(down_ready, i + 1)
                nc.vector.scalar_tensor_tensor(tile, dbank(t), sgd[:, :], tile, ALU.mult, ALU.add)\
                    .then_inc(res_ready, 1)

            def chunk(c, full):
                for e in range(1, ET):
                    hidden(c, e)
                    high(c, e - 1)
                high(c, ET - 1)
                if full:
                    hidden(c + 1, 0)
                for t in range(TPC):
                    result(c, t)

            dve.wait_ge(sgd_ready, 1)
            hidden(0, 0)
            with dve.Fori(0, NCH - 1) as c:
                chunk(c, True)
            chunk(NCH - 1, False)

        @block.gpsimd
        def _(pool):
            with pool.Fori(0, NCH) as c:
                for e in range(ET):
                    pool.wait_ge(h_high, c * ET + e + 1)
                    nc.gpsimd.tensor_tensor(hl[:, e, :], hid[:, e % 2, :], hh[:, e, :], ALU.subtract).then_inc(h_low, 1)


def build(nc, x, w_in_t, w_out_t, rms_w, ffn_t, cos_dram, sin_dram, ident_dram, half_consts, out):
    resid = nc.dram_tensor("resid_scratch", (S, D), F32, kind="Internal").ap()
    attn = nc.dram_tensor("attn_scratch", (S, C), F32, kind="Internal").ap()
    with nc.sbuf_tensor("raw", [P, NW], F32) as raw, nc.sbuf_tensor("ident_sb", [P, P], F32) as ident:
        with ExitStack() as ctx:
            sb = lambda name, shape, dt: ctx.enter_context(nc.sbuf_tensor(name, shape, dt))
            yh = sb("yh", [P, KT, S], F16)
            yl = sb("yl", [P, KT, S], F16)
            consts = sb("consts", [P, 4, P], F16)
            cos = sb("cos_sb", [P, TT, DH], F32)
            sin = sb("sin_sb", [P, TT, DH], F32)
            wraw = sb("wraw", [P, KT, GC], F32)
            ahead = [(ident[:, :], ident_dram),
                     (wraw[:, :, :], w_in_t[0].rearrange("(k p) n -> p k n", p=P)),
                     (consts[:, :, :], half_consts),
                     (cos[:, :, :], cos_dram.rearrange("(n p) d -> p n d", p=P)),
                     (sin[:, :, :], sin_dram.rearrange("(n p) d -> p n d", p=P))]
            normalise(nc, x, rms_w, resid, yh, yl, ident, ahead)
            attention(nc, w_in_t, w_out_t, attn, yh, yl, ident, consts, cos, sin, wraw, raw[:, :])
        with ExitStack() as ctx:
            sb = lambda name, shape, dt: ctx.enter_context(nc.sbuf_tensor(name, shape, dt))
            tern = sb("tern", [P, 3, NW], F16)
            scale = sb("tern_scale", [P, 3], F32)
            x2 = sb("x2", [P, TT, D], F32)
            xh = sb("xh", [P, KT, S], F16)
            xl = sb("xl", [P, KT, S], F16)
            output_projection(nc, raw, ffn_t, ident, attn, resid, tern, scale, x2, xh, xl)
            feed_forward(nc, tern, scale, x2, xh, xl, out)


def shape_constants():
    inv_freq = (np.float32(1.0) / np.float32(10000.0) ** (np.arange(0, DH, 2, dtype=np.float32) / np.float32(DH)))
    ang = np.arange(S, dtype=np.float32)[:, None] * inv_freq.astype(np.float32)[None, :]
    cos, sin = np.cos(ang).astype(np.float32), np.sin(ang).astype(np.float32)
    big = np.float16(30000.0)
    key, query = np.arange(P)[:, None], np.arange(P)[None, :]
    half = np.stack([np.eye(P), np.eye(P) * big, np.where(key > query, -big, 0), np.where(query > key, -big, 0)], axis=1)
    return (np.concatenate([cos, cos], 1), np.concatenate([-sin, sin], 1), np.eye(P, dtype=np.float32),
            half.astype(np.float16))


def kernel(L0_attn_x, L0_attn_w_in, L0_attn_w_out, L0_attn_rms_w, L0_ffn_W_up, L0_ffn_W_gate, L0_ffn_W_down):
    import concourse.bacc as bacc
    from concourse.bass_utils import run_bass_kernel_spmd

    w = np.asarray(L0_attn_w_in)
    nq, nk = C, GROUPS * DH
    by_group = np.concatenate([w[:nq].reshape(GROUPS, HG * DH, D), w[nq:nq + nk].reshape(GROUPS, DH, D),
                               w[nq + nk:].reshape(GROUPS, DH, D)], axis=1)
    by_group = np.concatenate([by_group, by_group[:1]])
    ffn_t = np.stack([np.asarray(m).T.reshape(-1, P, m.shape[0]).transpose(1, 0, 2).reshape(P, -1)
                      for m in (L0_ffn_W_up, L0_ffn_W_gate, L0_ffn_W_down)])
    cos, sin, ident, half = shape_constants()
    arrays = {
        "x": np.asarray(L0_attn_x), "w_in_t": by_group.transpose(0, 2, 1), "w_out_t": np.asarray(L0_attn_w_out).T,
        "rms_w": np.asarray(L0_attn_rms_w), "ffn_t": ffn_t, "cos": cos, "sin": sin, "ident": ident, "half_consts": half,
    }
    arrays = {n: np.ascontiguousarray(a) for n, a in arrays.items()}
    nc = bacc.Bacc("TRN2", target_bir_lowering=False, num_devices=1)
    args = [nc.dram_tensor(n, a.shape, mybir.dt.from_np(a.dtype), kind="ExternalInput").ap() for n, a in arrays.items()]
    out = nc.dram_tensor("out", (1, S, D), F32, kind="ExternalOutput").ap()
    build(nc, *args, out)
    return run_bass_kernel_spmd(nc, [arrays], core_ids=[0]).results[0]["out"]
```
